# Optimizing a Trainium2 kernel written in Bass

```python
import numpy as np
import jax
import jax.numpy as jnp

def _softmax(x, axis=-1):
    return jax.nn.softmax(x, axis=axis)

def _gelu(x):
    return jax.nn.gelu(x, approximate=True)

def _silu(x):
    return jax.nn.silu(x)

def _sigmoid(x):
    return jax.nn.sigmoid(x)

def _layernorm(x, axis=-1, eps=1e-05):
    m = jnp.mean(x, axis=axis, keepdims=True)
    v = jnp.var(x, axis=axis, keepdims=True)
    return (x - m) / jnp.sqrt(v + eps)

def _scatter_add(tgt, idx, src, axis=0):
    return tgt.at[idx].add(src)

def _segment_sum(src, seg, n):
    return jax.ops.segment_sum(src, seg, n)
kernel_name = 'mk_vit_tower_d1_tok_img1024_r4_e80b71'

def setup_inputs(seed: int=0):
    np.random.seed(seed)
    _w = jnp.asarray

    def _rec_inputs():
        import jax
        import jax.numpy as jnp
        _rk = jax.random.key(seed)
        x = -0.000356955 + 1 * jax.random.normal(jax.random.fold_in(_rk, 1), (64, 3, 128, 128), jnp.float32)
        return x
    x = _rec_inputs()

    def _L0_tok_setup():
        import jax, jax.numpy as jnp
        import numpy as np
        PH, PW = (16, 16)
        key = jax.random.key(seed)
        k1, k2 = jax.random.split(key)
        B, C, H, W_ = (128, 3, 224, 224)
        embed_dim = 256
        patch_dim = C * PH * PW
        x = jax.random.normal(k1, (B, C, H, W_), dtype=jnp.float32)
        W = jax.random.normal(k2, (embed_dim, patch_dim), dtype=jnp.float32) * 0.02
        b = jnp.zeros((embed_dim,), dtype=jnp.float32)
        return {'x': x, 'W': W, 'b': b}
    _L0_tok_all = _L0_tok_setup()
    _L0_tok_in = {k: v for k, v in _L0_tok_all.items() if k in ('W', 'b')}
    del _L0_tok_all

    def _L0_attn_setup():
        import jax, jax.numpy as jnp
        import numpy as np
        HEADS = 16
        DIM = 256
        SPARSITY = 0.1
        key = jax.random.key(seed)
        k1, k2, k3 = jax.random.split(key, 3)
        b, n, d = (2, 512, DIM)
        inner = HEADS * 64
        x = jax.random.normal(k1, (b, n, d), dtype=jnp.float32)
        W_qkv = jax.random.normal(k2, (3 * inner, d), dtype=jnp.float32) * d ** (-0.5)
        W_out = jax.random.normal(k3, (d, inner), dtype=jnp.float32) * inner ** (-0.5)
        b_out = jnp.zeros((d,), dtype=jnp.float32)
        return {'x': x, 'W_qkv': W_qkv, 'W_out': W_out, 'b_out': b_out}
    _L0_attn_all = _L0_attn_setup()
    _L0_attn_in = {k: v for k, v in _L0_attn_all.items() if k in ('W_qkv', 'W_out', 'b_out')}
    del _L0_attn_all

    def _L0_ffn_setup():
        import jax, jax.numpy as jnp
        import numpy as np
        from jax import lax
        T, B, I, M, O = (64, 64, 256, 256, 256)

        def _xavier(key, shape):
            fan_out, fan_in = shape
            limit = float(np.sqrt(6.0 / (fan_in + fan_out)))
            return jax.random.uniform(key, shape, jnp.float32, -limit, limit)
        key = jax.random.key(seed)
        ks = jax.random.split(key, 9)
        x = jax.random.normal(ks[0], (T, B, I), jnp.float32)
        return {'x': x, 'wf': _xavier(ks[1], (M, I)), 'uf': _xavier(ks[2], (M, M)), 'bf': jnp.zeros((M,), jnp.float32), 'wi': _xavier(ks[3], (M, I)), 'ui': _xavier(ks[4], (M, M)), 'bi': jnp.zeros((M,), jnp.float32), 'wc': _xavier(ks[5], (M, I)), 'uc': _xavier(ks[6], (M, M)), 'bc': jnp.zeros((M,), jnp.float32), 'wo': _xavier(ks[7], (O, I)), 'uo': _xavier(ks[8], (O, M)), 'bo': jnp.zeros((O,), jnp.float32), 'in_c': jnp.zeros((M,), jnp.float32)}
    _L0_ffn_all = _L0_ffn_setup()
    _L0_ffn_in = {k: v for k, v in _L0_ffn_all.items() if k in ('wf', 'uf', 'bf', 'wi', 'ui', 'bi', 'wc', 'uc', 'bc', 'wo', 'uo', 'bo', 'in_c')}
    del _L0_ffn_all
    return {'x': x, 'L0_tok_W': _L0_tok_in['W'], 'L0_tok_b': _L0_tok_in['b'], 'L0_attn_W_qkv': _L0_attn_in['W_qkv'], 'L0_attn_W_out': _L0_attn_in['W_out'], 'L0_attn_b_out': _L0_attn_in['b_out'], 'L0_ffn_wf': _L0_ffn_in['wf'], 'L0_ffn_uf': _L0_ffn_in['uf'], 'L0_ffn_bf': _L0_ffn_in['bf'], 'L0_ffn_wi': _L0_ffn_in['wi'], 'L0_ffn_ui': _L0_ffn_in['ui'], 'L0_ffn_bi': _L0_ffn_in['bi'], 'L0_ffn_wc': _L0_ffn_in['wc'], 'L0_ffn_uc': _L0_ffn_in['uc'], 'L0_ffn_bc': _L0_ffn_in['bc'], 'L0_ffn_wo': _L0_ffn_in['wo'], 'L0_ffn_uo': _L0_ffn_in['uo'], 'L0_ffn_bo': _L0_ffn_in['bo'], 'L0_ffn_in_c': _L0_ffn_in['in_c']}

def reference(x, L0_tok_W, L0_tok_b, L0_attn_W_qkv, L0_attn_W_out, L0_attn_b_out, L0_ffn_wf, L0_ffn_uf, L0_ffn_bf, L0_ffn_wi, L0_ffn_ui, L0_ffn_bi, L0_ffn_wc, L0_ffn_uc, L0_ffn_bc, L0_ffn_wo, L0_ffn_uo, L0_ffn_bo, L0_ffn_in_c):
    import jax
    import jax.numpy as jnp

    def _L0_tok_ref(x, W, b):
        import jax, jax.numpy as jnp
        import numpy as np
        PH, PW = (16, 16)
        B, C, H, Wd = x.shape
        nh, nw = (H // PH, Wd // PW)
        p = x.reshape(B, C, nh, PH, nw, PW).transpose(0, 2, 4, 1, 3, 5)
        p = p.reshape(B, nh * nw, C * PH * PW)
        return jnp.einsum('bnp,dp->bnd', p, W) + b

    def _L0_attn_ref(x, W_qkv, W_out, b_out):
        import jax, jax.numpy as jnp
        import numpy as np
        HEADS = 16
        DIM = 256
        SPARSITY = 0.1
        b, n, d = x.shape
        h = HEADS
        scale = d ** (-0.5)
        qkv = jnp.einsum('bnd,ed->bne', x, W_qkv)
        q, k, v = jnp.split(qkv, 3, axis=-1)

        def to_heads(t):
            return t.reshape(b, n, h, -1).transpose(0, 2, 1, 3)
        q, k, v = (to_heads(q), to_heads(k), to_heads(v))
        dots = jnp.einsum('bhid,bhjd->bhij', q, k) * scale
        mask_value = -jnp.finfo(dots.dtype).max
        k_top = max(1, int(SPARSITY * n))
        topk_vals, _ = jax.lax.top_k(dots, k_top)
        thresh = topk_vals[..., -1:]
        dots = jnp.where(dots >= thresh, dots, mask_value)
        v = jax.nn.relu(v)
        attn = jax.nn.softmax(dots, axis=-1)
        out = jnp.einsum('bhij,bhjd->bhid', attn, v)
        out = out.transpose(0, 2, 1, 3).reshape(b, n, -1)
        out = jnp.einsum('bne,de->bnd', out, W_out) + b_out
        return out

    def _L0_ffn_ref(x, wf, uf, bf, wi, ui, bi, wc, uc, bc, wo, uo, bo, in_c):
        import jax, jax.numpy as jnp
        import numpy as np
        from jax import lax
        T, B, I, M, O = (64, 64, 256, 256, 256)

        def _xavier(key, shape):
            fan_out, fan_in = shape
            limit = float(np.sqrt(6.0 / (fan_in + fan_out)))
            return jax.random.uniform(key, shape, jnp.float32, -limit, limit)
        batch = x.shape[1]
        c0 = jnp.broadcast_to(in_c, (batch, in_c.shape[0]))

        def step(c, xt):
            ft = jax.nn.sigmoid(xt @ wf.T + c @ uf.T + bf)
            it = jax.nn.sigmoid(xt @ wi.T + c @ ui.T + bi)
            gt = jnp.tanh(xt @ wc.T + c @ uc.T + bc)
            c = ft * c + it * gt
            return (c, None)
        c_final, _ = lax.scan(step, c0, x)
        h = jnp.tanh(jnp.einsum('tbi,oi->tbo', x, wo) + c_final @ uo.T + bo)
        return h
    h = _L0_tok_ref(x, L0_tok_W, L0_tok_b)
    h = h + _L0_attn_ref(_layernorm(h, axis=-1), L0_attn_W_qkv, L0_attn_W_out, L0_attn_b_out)
    h = h + _L0_ffn_ref(_layernorm(h, axis=-1), L0_ffn_wf, L0_ffn_uf, L0_ffn_bf, L0_ffn_wi, L0_ffn_ui, L0_ffn_bi, L0_ffn_wc, L0_ffn_uc, L0_ffn_bc, L0_ffn_wo, L0_ffn_uo, L0_ffn_bo, L0_ffn_in_c)
    return h

_drawn_inputs = setup_inputs


def setup_inputs(seed=0):
    import zlib

    import numpy as np

    out = dict(_drawn_inputs(seed))
    spreads = {'L0_tok_b': (0.0, 0.1),
     'L0_attn_b_out': (0.0, 0.1),
     'L0_ffn_bf': (0.0, 0.1),
     'L0_ffn_bi': (0.0, 0.1),
     'L0_ffn_bc': (0.0, 0.1),
     'L0_ffn_bo': (0.0, 0.1),
     'L0_ffn_in_c': (0.0, 0.8)}
    factors = {}
    for name, (base, spread) in spreads.items():
        noise = np.random.default_rng([zlib.crc32(name.encode()), seed]).standard_normal(out[name].shape)
        drawn = base * np.exp(spread * noise) if base else spread * noise
        out[name] = jnp.asarray(drawn.astype(out[name].dtype))
    for name, factor in factors.items():
        out[name] = (out[name] * factor).astype(out[name].dtype)
    return out
```

```python
import math
from contextlib import ExitStack

import concourse.bass as bass
from concourse import mybir

F32 = mybir.dt.float32
F16 = mybir.dt.float16
I32 = mybir.dt.int32
ALU = mybir.AluOpType
ACT = mybir.ActivationFunctionType

P = 128
IMAGES, TOKENS, DIM = 64, 64, 256
PAIRS = IMAGES // 2
PATCH = 3 * 16 * 16
XC = PATCH // P
HEADS, HD = 16, 64
INNER = HEADS * HD
HP = HEADS // 2
KD = DIM // P
GATES = 3 * DIM
GM = GATES // P
TOPK = max(1, int(0.1 * TOKENS))
EPS = 1e-5
SE = DIM ** -0.5 / 16.0
NEWTON = 3
RSQRT_BITS = float(0x5F3759DF)
VW = HD + 2

SW = 64.0
SQ = 4.0
SA = 4.0
SP = 256.0
SU = SW / 2

FIRST, LAST = -2, PAIRS + 1
LOOP_FROM, LOOP_TO = 3, PAIRS - 2


def build_program(nc, x, tok_w, tok_b, qkv_w, out_w, out_b, ffn_w, rec_w, gate_b, ffn_bo, in_c, out):
    with ExitStack() as ctx:
        def sb(name, shape, dt):
            return ctx.enter_context(nc.sbuf_tensor(name, shape, dt))

        def bank(name):
            return ctx.enter_context(nc.psum_tensor(name, [P, 512], F32))

        def sem(name):
            return ctx.enter_context(nc.semaphore(name))

        tokw = [sb(f"tokw_{s}", [P, XC, DIM], F16) for s in ("hi", "lo")]
        qkvw = [sb(f"qkvw_{s}", [P, KD, 3 * INNER], F16) for s in ("hi", "lo")]
        outw = [sb(f"outw_{s}", [P, HP, DIM], F16) for s in ("hi", "lo")]
        ffnw = [sb(f"ffnw_{s}", [P, KD, 4 * DIM], F16) for s in ("hi", "lo")]
        recw = [sb(f"recw_{s}", [P, KD, 4 * DIM], F16) for s in ("hi", "lo")]
        biasw = sb("biasw", [P, GATES], F16)
        bias_st = sb("bias_st", [33, GATES], F32)
        bias_hi = sb("bias_hi", [33, GATES], F16)
        tokb = sb("tokb", [P, DIM], F32)
        outb = sb("outb", [P, DIM], F32)
        ffnbo = sb("ffnbo", [P, DIM], F32)
        c0 = sb("c0", [P, KD], F32)
        ident = sb("ident", [P, P], F32)
        ones = sb("ones", [P, TOKENS], F16)
        h_all = sb("h_all", [P, PAIRS, DIM], F32)
        xo_all = sb("xo_all", [P, PAIRS, DIM], F32)
        xo_flat = xo_all[:, :, :].rearrange("p a d -> p (a d)")
        h_flat = h_all[:, :, :].rearrange("p a d -> p (a d)")
        tok_st = xo_flat[:, 0:XC * DIM]
        qkv_st = xo_flat[:, XC * DIM:XC * DIM + KD * 3 * INNER]
        tail = 8 * DIM
        out_st = h_flat[:, tail:tail + HP * DIM]
        ffn_st = h_flat[:, tail + HP * DIM:tail + HP * DIM + KD * 4 * DIM]
        rec_st = h_flat[:, tail + HP * DIM + KD * 4 * DIM:tail + HP * DIM + 2 * KD * 4 * DIM]
        xf = sb("xf", [P, XC * P], F32)
        xs = [sb(f"xs_{s}", [P, XC, P], F16) for s in ("hi", "lo")]
        z1 = sb("z1", [P, DIM], F32)
        z2 = sb("z2", [P, DIM], F32)
        st1 = sb("st1", [P, 6], F32)
        st2 = sb("st2", [P, 6], F32)
        mv1 = sb("mv1", [P, 2], F32)
        mv2 = sb("mv2", [P, 2], F32)
        rs1 = sb("rs1", [P, 1], F32)
        rs2 = sb("rs2", [P, 1], F32)
        nt = sb("nt", [P, 1], F32)
        z1t = [sb(f"z1t_{s}", [P, KD, P], F16) for s in ("hi", "lo")]
        z2t = [sb(f"z2t_{s}", [P, KD, P], F16) for s in ("hi", "lo")]
        qd = [sb(f"qd_{s}", [P, HP, 2, P], F16) for s in ("hi", "lo")]
        kt = [sb(f"kt_{s}", [P, HP, P], F16) for s in ("hi", "lo")]
        vn = [sb(f"vn_{s}", [P, HEADS, VW], F16) for s in ("hi", "lo")]
        top8 = [sb(f"top8_{n}", [P, 8, 8], F32) for n in range(2)]
        ebias = [sb(f"ebias_{n}", [P, 8], F32) for n in range(2)]
        keep = [sb(f"keep_{n}", [P, 512], F16) for n in range(2)]
        expo = [sb(f"expo_{n}", [P, 512], F32) for n in range(2)]
        wts = [sb(f"wts_{n}", [P, 512], F32) for n in range(2)]
        pd = [sb(f"pd_{s}", [P, 8, P], F16) for s in ("hi", "lo")]
        rden = sb("rden", [P, 4], F32)
        att = sb("att", [P, HEADS, HD], F32)
        att_t = [sb(f"att_t_{s}", [P, HP, P], F16) for s in ("hi", "lo")]
        tfi = sb("tfi", [P, 2 * P], F32)
        tg = sb("tg", [P, P], F32)
        fs = sb("fs", [P, P], F32)
        ig = sb("ig", [P, P], F32)
        state = sb("state", [P, KD * TOKENS], F32)
        state_h = [sb(f"state_{s}", [P, KD, TOKENS], F16) for s in ("hi", "lo")]
        state_d = [sb(f"state_d_{s}", [P, KD, 2, TOKENS], F16) for s in ("hi", "lo")]
        cub = sb("cub", [P, DIM], F32)
        zero = sb("zero", [P, TOKENS], F32)
        fin = sb("fin", [P, 2, 4 * DIM], F32)
        fin_t = sb("fin_t", [P, 2, 4 * DIM], F32)

        p_gate = [bank("p_gate0"), bank("p_gate1")]
        p_a, p_b = bank("p_a"), bank("p_b")
        p_s = [bank("p_s0"), bank("p_s1")]
        p_t = bank("p_t")
        p_av = bank("p_av")

        ld_tok, ld_qkv, ld_out = sem("ld_tok"), sem("ld_qkv"), sem("ld_out")
        ld_ffn, ld_rec, ld_small = sem("ld_ffn"), sem("ld_rec"), sem("ld_small")
        ld_x = sem("ld_x")
        passed = sem("passed")
        made = sem("made")
        zeroed = sem("zeroed")
        ident_ok = sem("ident_ok")
        wh = sem("wh")
        wl = sem("wl")
        setup_ok = sem("setup_ok")
        x_hi, x_lo = sem("x_hi"), sem("x_lo")
        tok_done, h1_ok, ln1, z1_ok = sem("tok_done"), sem("h1_ok"), sem("ln1"), sem("z1_ok")
        rstd1, rstd2 = sem("rstd1"), sem("rstd2")
        res_ok = sem("res_ok")
        z1t_done, z1t_hi, z1t_lo = sem("z1t_done"), sem("z1t_hi"), sem("z1t_lo")
        fills = ("q0", "q1", "k0", "k1", "v0", "v1")
        f_done = {n: sem(f"{n}_done") for n in fills}
        f_hi = {n: sem(f"{n}_hi") for n in fills}
        f_lo = {n: sem(f"{n}_lo") for n in fills}
        s_done = [sem(f"s_done{n}") for n in range(2)]
        max_ok = [sem(f"max_ok{n}") for n in range(2)]
        ebias_ok = [sem(f"ebias_ok{n}") for n in range(2)]
        keep_ok = [sem(f"keep_ok{n}") for n in range(2)]
        exp_ok = [sem(f"exp_ok{n}") for n in range(2)]
        wts_ok = [sem(f"wts_ok{n}") for n in range(2)]
        pt_done = [sem(f"pt_done{n}") for n in range(2)]
        pt_hi = [sem(f"pt_hi{n}") for n in range(2)]
        pt_lo = [sem(f"pt_lo{n}") for n in range(2)]
        av_done = [sem(f"av_done{n}") for n in range(4)]
        rden_ok = [sem(f"rden_ok{n}") for n in range(4)]
        att_ok = [sem(f"att_ok{n}") for n in range(4)]
        at_done = [sem(f"at_done{n}") for n in range(2)]
        at_hi = [sem(f"at_hi{n}") for n in range(2)]
        at_lo = [sem(f"at_lo{n}") for n in range(2)]
        y_done, h2_ok, ln2, z2_ok = sem("y_done"), sem("h2_ok"), sem("ln2"), sem("z2_ok")
        z2t_done, z2t_hi, z2t_lo = sem("z2t_done"), sem("z2t_hi"), sem("z2t_lo")
        gx_done, xo_done, xo_ok = sem("gx_done"), sem("xo_done"), sem("xo_ok")
        rec_done = [sem(f"rec_done{n}") for n in range(2)]
        tfi_ok = [sem(f"tfi_ok{n}") for n in range(2)]
        tg_ok = [sem(f"tg_ok{n}") for n in range(2)]
        rec_step = [sem(f"rec_step{n}") for n in range(2)]
        st_ok = [sem(f"st_ok{n}") for n in range(2)]
        st0 = sem("st0")
        dup_ok, cu_done, cub_ok = sem("dup_ok"), sem("cu_done"), sem("cub_ok")
        fin_in, fin_tanh, fin_ok = sem("fin_in"), sem("fin_tanh"), sem("fin_ok")
        stored = [sem(f"stored{n}") for n in range(2)]

        def valid(p):
            return not isinstance(p, int) or 0 <= p < PAIRS

        turns_a = [(f_lo["k1"], 1), (f_lo["q1"], 1), (f_lo["q0"], 1), (f_lo["v1"], 1)]
        turns_b = [(h2_ok, -1), (f_lo["k0"], 1), (h1_ok, 2), (f_lo["v0"], 1), (xo_ok, -1)]
        turns_t = [(z1t_lo, 1), (pt_lo[0], 0), (z2t_lo, -1), (pt_lo[1], 0), (at_lo[0], 0), (at_lo[1], 0)]
        turns_v = [(att_ok[0], 0), (att_ok[1], 0), (att_ok[2], 0), (att_ok[3], 0)]
        home = {n: (p_a, turns_a) for n in ("k1", "q1", "q0", "v1")}
        home.update({n: (p_b, turns_b) for n in ("project", "k0", "embed", "v0", "out_x")})

        def bank_free(eng, turns, reader, i):
            at = [t[0] is reader for t in turns].index(True)
            n = i
            while True:
                at -= 1
                if at < 0:
                    at, n = len(turns) - 1, n - 1
                if isinstance(n, int) and n < FIRST:
                    return
                s, lag = turns[at]
                if valid(n + lag):
                    eng.wait_ge(s, n + lag + 1)
                    return

        def wait_alone(eng, s, value):
            eng.wait_ge(s, value)
            eng.sem_inc(passed, 1)

        def iterate(eng, body, before=None):
            for i in range(FIRST, LOOP_FROM):
                if before and i in before:
                    before[i]()
                body(i)
            with eng.Fori(LOOP_FROM, LOOP_TO) as i:
                body(i)
            for i in range(LOOP_TO, LAST + 1):
                body(i)

        block = ctx.enter_context(nc.Block())

        @block.sync
        def _(eng):
            eng.dma_start(tok_st, tok_w).then_inc(ld_tok, 16)
            eng.dma_start(xf[:], x[0]).then_inc(ld_x, 16)
            eng.dma_start(tokb[:], tok_b.partition_broadcast(P)).then_inc(ld_small, 16)
            eng.dma_start(outb[:], out_b.partition_broadcast(P)).then_inc(ld_small, 16)
            eng.dma_start(ffnbo[:], ffn_bo.partition_broadcast(P)).then_inc(ld_small, 16)
            eng.dma_start(c0[:], in_c).then_inc(ld_small, 16)
            eng.dma_start(bias_st[0:1, :], gate_b).then_inc(ld_small, 16)
            eng.dma_start(bias_st[32:33, :], gate_b).then_inc(ld_small, 16)
            eng.dma_start(qkv_st, qkv_w).then_inc(ld_qkv, 16)
            eng.dma_start(out_st, out_w).then_inc(ld_out, 16)
            eng.dma_start(ffn_st, ffn_w).then_inc(ld_ffn, 16)
            eng.dma_start(rec_st, rec_w).then_inc(ld_rec, 16)
            with eng.Fori(1, PAIRS) as p:
                eng.wait_ge(x_hi, p)
                eng.wait_ge(x_lo, p)
                eng.dma_start(xf[:], x[p]).then_inc(ld_x, 16)
            for n in range(PAIRS // 4):
                eng.wait_ge(fin_ok, n + 1)
                eng.dma_start(out[4 * n:4 * n + 4].rearrange("a p d -> p a d"),
                              fin[:, n % 2, :].rearrange("p (a d) -> p a d", a=4)).then_inc(stored[n % 2], 16)
            for n in range(2):
                eng.wait_ge(stored[n], 16 * (PAIRS // 8))

        @block.gpsimd
        def _(eng):
            eng.memset(ident[:], 0.0).then_inc(made, 1)
            eng.wait_ge(made, 1)
            eng.affine_select(out=ident[:], in_=ident[:], compare_op=ALU.not_equal, fill=1.0, base=0,
                              pattern=[[-1, P]], channel_multiplier=1).then_inc(ident_ok, 1)
            eng.wait_ge(ld_small, 96)

            def patches_lo(i):
                eng.wait_ge(x_hi, i + 3)
                eng.tensor_tensor(xs[1][:].rearrange("p c t -> p (c t)"), xf[:],
                                  xs[0][:].rearrange("p c t -> p (c t)"), ALU.subtract).then_inc(x_lo, 1)

            def add_bias(i):
                eng.wait_ge(z1_ok, i + 3)
                eng.tensor_tensor(h_all[:, i + 2, :], h_all[:, i + 2, :], outb[:], ALU.add).then_inc(res_ok, 1)

            def exp_bias(i, hf):
                wait_alone(eng, max_ok[hf], i + 1)
                eng.tensor_scalar(ebias[hf][:], top8[hf][:, :, 0], -SE, None, ALU.mult).then_inc(ebias_ok[hf], 1)

            def inverse_deviation(p, mv, rs, chain, ok):
                var, y, t = mv[:, 1:2], rs[:], nt[:]
                at = 3 * NEWTON * p
                wait_alone(eng, chain, 4 * p + 4)
                for n in range(NEWTON):
                    if n:
                        wait_alone(eng, ok, at + 3 * n)
                    eng.tensor_scalar(t, y, y, var, ALU.mult, ALU.mult).then_inc(ok, 1)
                    wait_alone(eng, ok, at + 3 * n + 1)
                    eng.tensor_scalar(t, t, -0.5, 1.5, ALU.mult, ALU.add).then_inc(ok, 1)
                    wait_alone(eng, ok, at + 3 * n + 2)
                    eng.tensor_tensor(y, y, t, ALU.mult).then_inc(ok, 1)

            def mask(i, hf):
                eng.wait_ge(exp_ok[hf], i + 1)
                eng.wait_ge(keep_ok[hf], i + 1)
                eng.tensor_tensor(wts[hf][:], expo[hf][:], keep[hf][:], ALU.mult).then_inc(wts_ok[hf], 1)

            def body(i):
                if valid(i):
                    exp_bias(i, 0)
                if valid(i + 2):
                    patches_lo(i)
                if valid(i):
                    mask(i, 0)
                    exp_bias(i, 1)
                if valid(i - 1):
                    inverse_deviation(i - 1, mv2, rs2, ln2, rstd2)
                if valid(i):
                    mask(i, 1)
                if valid(i + 2):
                    inverse_deviation(i + 2, mv1, rs1, ln1, rstd1)
                    add_bias(i)
            iterate(eng, body)

        @block.tensor
        def _(eng):
            def mm3(o, stat, mov, start, stop, skip=False):
                sh, sl = stat
                mh, ml = mov
                eng.matmul(o, sh, mh, start=start, stop=False, skip_group_check=skip)
                eng.matmul(o, sh, ml, start=False, stop=False, skip_group_check=skip)
                return eng.matmul(o, sl, mh, start=False, stop=stop, skip_group_check=skip)

            def part(pair, f):
                return [f(t) for t in pair]

            def embed(i):
                p = i + 2
                eng.wait_ge(x_hi, p + 1)
                eng.wait_ge(x_lo, p + 1)
                bank_free(eng, home["embed"][1], h1_ok, i)
                for c in range(XC):
                    last = mm3(home["embed"][0][:, 0:DIM], part(xs, lambda t: t[:, c, :]), part(tokw, lambda t: t[:, c, :]),
                               c == 0, c == XC - 1)
                last.then_inc(tok_done, 1)

            def turn_z(i, z, ready, turns, reader, done, p):
                eng.wait_ge(ready, p + 1)
                bank_free(eng, turns, reader, i)
                for k in range(KD):
                    last = eng.transpose(p_t[:, k * P:(k + 1) * P], z[:, k * P:(k + 1) * P], ident[:])
                last.then_inc(done, 1)

            def fill(i, name):
                p = i + 1
                hf = int(name[1])
                bnk, turns = home[name]
                if name == "k1":
                    eng.wait_ge(z1t_lo, p + 1)
                bank_free(eng, turns, f_lo[name], i)
                if name[0] == "v":
                    o = 2 * INNER + 512 * hf
                    for k in range(KD):
                        last = mm3(bnk[:, :], part(z1t, lambda t: t[:, k, :]),
                                   part(qkvw, lambda t: t[:, k, o:o + 512]), k == 0, k == KD - 1)
                else:
                    o = INNER * "qk".index(name[0]) + 512 * hf
                    for c in range(4):
                        for k in range(KD):
                            last = mm3(bnk[:, c * P:(c + 1) * P],
                                       part(qkvw, lambda t: t[:, k, o + c * P:o + (c + 1) * P]),
                                       part(z1t, lambda t: t[:, k, :]), k == 0, k == KD - 1)
                last.then_inc(f_done[name], 1)

            def scores(i, hf):
                eng.wait_ge(f_lo[f"q{hf}"], i + 1)
                eng.wait_ge(f_lo[f"k{hf}"], i + 1)
                if not isinstance(i, int) or i > 0:
                    eng.wait_ge(exp_ok[hf], i)
                for c in range(4):
                    for m in range(2):
                        last = mm3(p_s[hf][:, (2 * c + m) * 64:(2 * c + m + 1) * 64],
                                   part(qd, lambda t: t[:, 4 * hf + c, m, :]),
                                   part(kt, lambda t: t[:, 4 * hf + c, 64 * m:64 * m + 64]), True, True)
                last.then_inc(s_done[hf], 1)

            def turn_weights(i, hf):
                eng.wait_ge(wts_ok[hf], i + 1)
                bank_free(eng, turns_t, pt_lo[hf], i)
                for c in range(4):
                    last = eng.transpose(p_t[:, c * P:(c + 1) * P], wts[hf][:, c * P:(c + 1) * P], ident[:])
                last.then_inc(pt_done[hf], 1)

            def attend(i, qr):
                hf = qr // 2
                eng.wait_ge(pt_lo[hf], i + 1)
                eng.wait_ge(f_lo[f"v{hf}"], i + 1)
                bank_free(eng, turns_v, att_ok[qr], i)
                for n in range(4):
                    head = 4 * qr + n
                    last = mm3(p_av[:, n * VW:(n + 1) * VW], part(pd, lambda t: t[:, head % 8, :]),
                               part(vn, lambda t: t[:, head, :]), True, True)
                last.then_inc(av_done[qr], 1)

            def turn_att(i, hf):
                eng.wait_ge(att_ok[2 * hf + 1], i + 1)
                bank_free(eng, turns_t, at_lo[hf], i)
                for c in range(4):
                    j = 4 * hf + c
                    last = eng.transpose(p_t[:, c * P:(c + 1) * P],
                                         att[:, 2 * j:2 * j + 2, :].rearrange("p h d -> p (h d)"), ident[:])
                last.then_inc(at_done[hf], 1)

            def project(i):
                p = i - 1
                eng.wait_ge(at_lo[0], p + 1)
                eng.wait_ge(at_lo[1], p + 1)
                bank_free(eng, home["project"][1], h2_ok, i)
                for j in range(HP):
                    last = mm3(home["project"][0][:, 0:DIM], part(att_t, lambda t: t[:, j, :]),
                               part(outw, lambda t: t[:, j, :]), j == 0, j == HP - 1)
                last.then_inc(y_done, 1)

            def gates_x(i):
                p = i - 1
                eng.wait_ge(z2t_lo, p + 1)
                if not isinstance(p, int) or p > 0:
                    for s in range(2):
                        eng.wait_ge(tg_ok[s], p)
                for m in range(GM):
                    for s in range(2):
                        eng.matmul(p_gate[s][:, m * 64:m * 64 + 64], biasw[:, m * P:(m + 1) * P], ones[:],
                                   start=(m == 0), stop=False, skip_group_check=True)
                    for k in range(KD):
                        for wgt, zz in ((0, 0), (0, 1), (1, 0)):
                            for s in range(2):
                                last = eng.matmul(p_gate[s][:, m * 64:m * 64 + 64],
                                                  ffnw[wgt][:, k, m * P:(m + 1) * P],
                                                  z2t[zz][:, k, 64 * s:64 * s + 64],
                                                  start=False, stop=False, skip_group_check=True)
                last.then_inc(gx_done, 1)

            def out_x(i):
                bank_free(eng, home["out_x"][1], xo_ok, i)
                for k in range(KD):
                    last = mm3(home["out_x"][0][:, 0:DIM], part(z2t, lambda t: t[:, k, :]),
                               part(ffnw, lambda t: t[:, k, GATES:GATES + DIM]), k == 0, k == KD - 1)
                last.then_inc(xo_done, 1)

            def recur(p, s):
                if s == 1:
                    eng.wait_ge(st_ok[0], p + 1)
                elif isinstance(p, int) and p == 0:
                    eng.wait_ge(setup_ok, 1)
                else:
                    eng.wait_ge(st_ok[1], p)
                for m in range(GM):
                    for k in range(KD):
                        last = mm3(p_gate[s][:, m * 64:m * 64 + 64],
                                   part(recw, lambda t: t[:, k, m * P:(m + 1) * P]),
                                   part(state_h, lambda t: t[:, k, :]), False, m == GM - 1 and k == KD - 1, True)
                last.then_inc(rec_done[s], 1)

            def body(i):
                if valid(i):
                    scores(i, 0)
                if valid(i + 1):
                    turn_z(i, z1, z1_ok, turns_t, z1t_lo, z1t_done, i + 1)
                if valid(i - 1):
                    project(i)
                if valid(i):
                    scores(i, 1)
                if valid(i + 1):
                    fill(i, "k1")
                    fill(i, "k0")
                if valid(i):
                    turn_weights(i, 0)
                if valid(i + 1):
                    fill(i, "q1")
                if valid(i + 2):
                    embed(i)
                if valid(i - 2):
                    recur(i - 2, 1)
                if valid(i):
                    attend(i, 0)
                if valid(i - 1):
                    turn_z(i, z2, z2_ok, turns_t, z2t_lo, z2t_done, i - 1)
                if valid(i + 1):
                    fill(i, "q0")
                if valid(i):
                    attend(i, 1)
                    turn_weights(i, 1)
                if valid(i - 1):
                    gates_x(i)
                if valid(i + 1):
                    fill(i, "v0")
                if valid(i):
                    attend(i, 2)
                    turn_att(i, 0)
                if valid(i - 1):
                    recur(i - 1, 0)
                if valid(i):
                    attend(i, 3)
                if valid(i + 1):
                    fill(i, "v1")
                if valid(i):
                    turn_att(i, 1)
                if valid(i - 1):
                    out_x(i)

            eng.wait_ge(ident_ok, 1)
            eng.wait_ge(wl, 1)
            before = {-1: lambda: eng.wait_ge(wl, 2),
                      0: lambda: (eng.wait_ge(wl, 6), eng.wait_ge(zeroed, 9))}
            iterate(eng, body, before)
            eng.wait_ge(dup_ok, 2)
            for k in range(KD):
                last = mm3(p_a[:, 0:DIM], part(state_d, lambda t: t[:, k, :, :].rearrange("p a t -> p (a t)")),
                           part(recw, lambda t: t[:, k, GATES:GATES + DIM]), k == 0, k == KD - 1)
            last.then_inc(cu_done, 1)

        @block.scalar
        def _(eng):
            def weights_hi(st, pair, scale, loaded):
                eng.wait_ge(loaded, 16)
                eng.activation(flat(pair[0]), st, ACT.Copy, scale=scale).then_inc(wh, 1)

            def flat(t):
                return t[:].rearrange("p a b -> p (a b)")

            def patches_hi(i):
                p = i + 2
                eng.wait_ge(ld_x, 16 * (p + 1))
                if not isinstance(p, int) or p > 0:
                    eng.wait_ge(tok_done, p)
                eng.activation(flat(xs[0]), xf[:], ACT.Copy).then_inc(x_hi, 1)

            def fill_hi(i, name):
                p = i + 1
                hf = int(name[1])
                src = home[name][0]
                eng.wait_ge(f_done[name], p + 1)
                if name[0] == "q":
                    for u in range(2):
                        r = slice(64 * u, 64 * u + 64)
                        last = eng.activation(
                            qd[0][r, 4 * hf:4 * hf + 4, :, r].rearrange("p c m t -> p (c m) t"),
                            src[r, :].rearrange("p (c t) -> p c t", t=64), ACT.Copy, scale=SQ / SW)
                    last.then_inc(f_hi[name], 1)
                elif name[0] == "k":
                    eng.activation(kt[0][:, 4 * hf:4 * hf + 4, :].rearrange("p c t -> p (c t)"), src[:, :],
                                   ACT.Copy, scale=SQ / SW).then_inc(f_hi[name], 1)
                else:
                    eng.activation(vn[0][:, 8 * hf:8 * hf + 8, 0:HD], src[:, :].rearrange("p (h d) -> p h d", d=HD),
                                   ACT.Relu).then_inc(f_hi[name], 1)

            def exponentials(i, hf):
                eng.wait_ge(keep_ok[hf], i + 1)
                eng.wait_ge(ebias_ok[hf], i + 1)
                for u in range(8):
                    last = eng.activation(expo[hf][:, 64 * u:64 * u + 64], p_s[hf][:, 64 * u:64 * u + 64], ACT.Exp,
                                          bias=ebias[hf][:, u:u + 1], scale=SE)
                last.then_inc(exp_ok[hf], 1)

            def weights_t_hi(i, hf):
                eng.wait_ge(pt_done[hf], i + 1)
                for u in range(2):
                    r = slice(64 * u, 64 * u + 64)
                    last = eng.activation(pd[0][r, :, r], p_t[r, :].rearrange("p (h t) -> p h t", t=64),
                                          ACT.Copy, scale=SP)
                last.then_inc(pt_hi[hf], 1)

            def att_hi(p, hf):
                eng.wait_ge(at_done[hf], p + 1)
                eng.activation(att_t[0][:, 4 * hf:4 * hf + 4, :].rearrange("p c t -> p (c t)"), p_t[:, :],
                               ACT.Copy).then_inc(at_hi[hf], 1)

            def z_hi(p, zt, done, ok):
                eng.wait_ge(done, p + 1)
                eng.activation(flat(zt[0]), p_t[:, 0:DIM], ACT.Copy).then_inc(ok, 1)

            def gate_tanh(p, s):
                eng.wait_ge(rec_done[s], p + 1)
                if s == 1:
                    eng.wait_ge(st_ok[0], p + 1)
                elif not isinstance(p, int) or p > 0:
                    eng.wait_ge(st_ok[1], p)
                eng.activation(tfi[:], p_gate[s][:, 0:2 * P], ACT.Tanh, scale=0.5 / SW).then_inc(tfi_ok[s], 1)
                eng.activation(tg[:], p_gate[s][:, 2 * P:3 * P], ACT.Tanh, scale=1 / SW).then_inc(tg_ok[s], 1)

            def out_x_copy(i):
                eng.wait_ge(xo_done, i)
                eng.activation(xo_all[:, i - 1, :], home["out_x"][0][:, 0:DIM], ACT.Copy, scale=1 / SW).then_inc(xo_ok, 1)

            def body(i):
                if valid(i + 2):
                    patches_hi(i)
                if valid(i + 1):
                    z_hi(i + 1, z1t, z1t_done, z1t_hi)
                if valid(i):
                    exponentials(i, 0)
                if valid(i + 1):
                    fill_hi(i, "k1")
                    fill_hi(i, "k0")
                if valid(i):
                    weights_t_hi(i, 0)
                if valid(i + 1):
                    fill_hi(i, "q1")
                if valid(i):
                    exponentials(i, 1)
                if valid(i - 2):
                    gate_tanh(i - 2, 1)
                if valid(i - 1):
                    z_hi(i - 1, z2t, z2t_done, z2t_hi)
                if valid(i):
                    weights_t_hi(i, 1)
                if valid(i + 1):
                    fill_hi(i, "q0")
                    fill_hi(i, "v0")
                if valid(i):
                    att_hi(i, 0)
                if valid(i - 1):
                    gate_tanh(i - 1, 0)
                if valid(i):
                    att_hi(i, 1)
                if valid(i + 1):
                    fill_hi(i, "v1")
                if valid(i - 1):
                    out_x_copy(i)

            def rest_hi():
                weights_hi(out_st, outw, SW, ld_out)
                weights_hi(ffn_st, ffnw, SW, ld_ffn)
                weights_hi(rec_st, recw, SU, ld_rec)
                eng.wait_ge(ld_small, 96)
                eng.wait_ge(zeroed, 9)
                eng.activation(bias_hi[32:33, :], bias_st[32:33, :], ACT.Copy, scale=SW)
                eng.activation(biasw[0:1, :], bias_st[0:1, :], ACT.Copy, scale=SW).then_inc(wh, 1)
                eng.wait_ge(wl, 6)

            weights_hi(tok_st, tokw, SW, ld_tok)
            before = {-1: lambda: (weights_hi(qkv_st, qkvw, SW, ld_qkv), eng.wait_ge(zeroed, 9)), 0: rest_hi}
            iterate(eng, body, before)
            for n in range(PAIRS // 4):
                eng.wait_ge(fin_in, n + 1)
                if n >= 2:
                    eng.wait_ge(fin_ok, n - 1)
                eng.activation(fin_t[:, n % 2, :], fin[:, n % 2, :], ACT.Tanh).then_inc(fin_tanh, 1)

        @block.vector
        def _(eng):
            def flat(t):
                return t[:].rearrange("p a b -> p (a b)")

            def lo(o, src, scale, hi, op=ALU.mult):
                return eng.scalar_tensor_tensor(out=o, in0=src, scalar=scale, in1=hi, op0=op, op1=ALU.subtract)

            def weights_lo(st, pair, scale, n):
                eng.wait_ge(wh, n)
                lo(flat(pair[1]), st, scale, flat(pair[0])).then_inc(wl, 1)

            def statistics(p, h_ok, h, st, mv, rs, chain):
                wait_alone(eng, h_ok, p + 1)
                eng.bn_stats(st[:], h).then_inc(chain, 1)
                wait_alone(eng, chain, 4 * p + 1)
                eng.bn_aggr(mv[:], st[:]).then_inc(chain, 1)
                eng.wait_ge(chain, 4 * p + 2)
                eng.tensor_scalar(mv[:, 1:2], mv[:, 1:2], EPS, None, ALU.add).then_inc(chain, 1)
                eng.wait_ge(chain, 4 * p + 3)
                eng.tensor_scalar(rs[:].bitcast(I32), mv[:, 1:2].bitcast(I32), -0.5, RSQRT_BITS,
                                  ALU.mult, ALU.add).then_inc(chain, 1)

            def normal(p, mv, rs, z, rstd, z_ok):
                eng.wait_ge(rstd, 3 * NEWTON * (p + 1))
                eng.tensor_scalar(z[:], h_all[:, p, :], mv[:, 0:1], rs[:], ALU.subtract, ALU.mult).then_inc(z_ok, 1)

            def embed_out(i):
                p = i + 2
                eng.wait_ge(tok_done, p + 1)
                eng.scalar_tensor_tensor(out=h_all[:, p, :], in0=home["embed"][0][:, 0:DIM], scalar=1 / SW, in1=tokb[:],
                                         op0=ALU.mult, op1=ALU.add).then_inc(h1_ok, 1)
                statistics(p, h1_ok, h_all[:, p, :], st1, mv1, rs1, ln1)

            def project_out(i):
                p = i - 1
                eng.wait_ge(y_done, p + 1)
                eng.wait_ge(res_ok, p + 1)
                eng.scalar_tensor_tensor(out=h_all[:, p, :], in0=home["project"][0][:, 0:DIM], scalar=1 / (SW * SA),
                                         in1=h_all[:, p, :], op0=ALU.mult, op1=ALU.add).then_inc(h2_ok, 1)
                statistics(p, h2_ok, h_all[:, p, :], st2, mv2, rs2, ln2)

            def z_lo(p, zt, hi_ok, ok):
                eng.wait_ge(hi_ok, p + 1)
                eng.tensor_tensor(flat(zt[1]), p_t[:, 0:DIM], flat(zt[0]), ALU.subtract).then_inc(ok, 1)

            def fill_lo(i, name):
                p = i + 1
                hf = int(name[1])
                src = home[name][0]
                eng.wait_ge(f_hi[name], p + 1)
                if name[0] == "q":
                    for u in range(2):
                        r = slice(64 * u, 64 * u + 64)
                        o, hi = (t[r, 4 * hf:4 * hf + 4, :, r].rearrange("p c m t -> p (c m) t")
                                 for t in (qd[1], qd[0]))
                        last = lo(o, src[r, :].rearrange("p (c t) -> p c t", t=64), SQ / SW, hi)
                    last.then_inc(f_lo[name], 1)
                elif name[0] == "k":
                    o, hi = (t[:, 4 * hf:4 * hf + 4, :].rearrange("p c t -> p (c t)") for t in (kt[1], kt[0]))
                    lo(o, src[:, :], SQ / SW, hi).then_inc(f_lo[name], 1)
                else:
                    o, hi = (t[:, 8 * hf:8 * hf + 8, 0:HD] for t in (vn[1], vn[0]))
                    lo(o, src[:, :].rearrange("p (h d) -> p h d", d=HD), 0.0, hi, ALU.max).then_inc(f_lo[name], 1)

            def largest(i, hf):
                wait_alone(eng, s_done[hf], i + 1)
                for u in range(8):
                    last = eng.max(top8[hf][:, u, :], p_s[hf][:, 64 * u:64 * u + 64])
                last.then_inc(max_ok[hf], 1)

            def select(i, hf):
                eng.wait_ge(max_ok[hf], i + 1)
                eng.tensor_tensor(keep[hf][:].rearrange("p (u k) -> p u k", u=8),
                                  p_s[hf][:, :].rearrange("p (u k) -> p u k", u=8),
                                  top8[hf][:, :, TOPK - 1:TOPK].broadcast_to([P, 8, 64]),
                                  ALU.is_ge).then_inc(keep_ok[hf], 1)

            def weights_t_lo(i, hf):
                eng.wait_ge(pt_hi[hf], i + 1)
                for u in range(2):
                    r = slice(64 * u, 64 * u + 64)
                    last = lo(pd[1][r, :, r], p_t[r, :].rearrange("p (h t) -> p h t", t=64), SP, pd[0][r, :, r])
                last.then_inc(pt_lo[hf], 1)

            def normalise(i, qr):
                eng.wait_ge(av_done[qr], i + 1)
                av = p_av[:, 0:4 * VW].rearrange("p (h w) -> p h w", w=VW)
                eng.reciprocal(rden[:], av[:, :, HD]).then_inc(rden_ok[qr], 1)
                eng.wait_ge(rden_ok[qr], i + 1)
                eng.tensor_tensor(att[:, 4 * qr:4 * qr + 4, :], av[:, :, 0:HD],
                                  rden[:].unsqueeze(2).broadcast_to([P, 4, HD]), ALU.mult).then_inc(att_ok[qr], 1)

            def att_lo(p, hf):
                eng.wait_ge(at_hi[hf], p + 1)
                o, hi = (t[:, 4 * hf:4 * hf + 4, :].rearrange("p c t -> p (c t)") for t in (att_t[1], att_t[0]))
                eng.tensor_tensor(o, p_t[:, :], hi, ALU.subtract).then_inc(at_lo[hf], 1)

            def update(p, s):
                eng.wait_ge(tfi_ok[s], p + 1)
                eng.scalar_tensor_tensor(out=fs[:], in0=tfi[:, 0:P], scalar=1.0, in1=state[:],
                                         op0=ALU.add, op1=ALU.mult).then_inc(rec_step[s], 1)
                eng.wait_ge(tg_ok[s], p + 1)
                eng.scalar_tensor_tensor(out=ig[:], in0=tfi[:, P:2 * P], scalar=1.0, in1=tg[:],
                                         op0=ALU.add, op1=ALU.mult).then_inc(rec_step[s], 1)
                eng.wait_ge(rec_step[s], 4 * p + 2)
                eng.scalar_tensor_tensor(out=state[:], in0=fs[:], scalar=0.5, in1=ig[:],
                                         op0=ALU.mult, op1=ALU.add).then_inc(rec_step[s], 1)
                eng.wait_ge(rec_step[s], 4 * p + 3)
                eng.tensor_copy(flat(state_h[0]), state[:]).then_inc(rec_step[s], 1)
                eng.wait_ge(rec_step[s], 4 * p + 4)
                eng.tensor_tensor(flat(state_h[1]), state[:], flat(state_h[0]), ALU.subtract).then_inc(st_ok[s], 1)

            def body(i):
                if valid(i):
                    largest(i, 0)
                    select(i, 0)
                if valid(i + 1):
                    z_lo(i + 1, z1t, z1t_hi, z1t_lo)
                if valid(i - 1):
                    project_out(i)
                if valid(i):
                    largest(i, 1)
                if valid(i + 1):
                    fill_lo(i, "k1")
                if valid(i):
                    select(i, 1)
                if valid(i + 1):
                    fill_lo(i, "k0")
                if valid(i):
                    weights_t_lo(i, 0)
                if valid(i - 1):
                    normal(i - 1, mv2, rs2, z2, rstd2, z2_ok)
                if valid(i + 1):
                    fill_lo(i, "q1")
                if valid(i):
                    normalise(i, 0)
                if valid(i - 1):
                    z_lo(i - 1, z2t, z2t_hi, z2t_lo)
                if valid(i + 2):
                    embed_out(i)
                if valid(i - 2):
                    update(i - 2, 1)
                if valid(i):
                    normalise(i, 1)
                    weights_t_lo(i, 1)
                if valid(i + 1):
                    fill_lo(i, "q0")
                if valid(i):
                    normalise(i, 2)
                if valid(i + 1):
                    fill_lo(i, "v0")
                if valid(i + 2):
                    normal(i + 2, mv1, rs1, z1, rstd1, z1_ok)
                if valid(i):
                    att_lo(i, 0)
                    normalise(i, 3)
                if valid(i - 1):
                    update(i - 1, 0)
                if valid(i):
                    att_lo(i, 1)
                if valid(i + 1):
                    fill_lo(i, "v1")

            def rest_lo():
                weights_lo(out_st, outw, SW, 3)
                weights_lo(ffn_st, ffnw, SW, 4)
                weights_lo(rec_st, recw, SU, 5)
                eng.wait_ge(wh, 6)
                lo(biasw[32:33, :], bias_st[32:33, :], SW, bias_hi[32:33, :]).then_inc(wl, 1)
                for k in range(KD):
                    last = eng.tensor_scalar(state[:, k * TOKENS:(k + 1) * TOKENS], zero[:, 0:TOKENS],
                                             c0[:, k:k + 1], 2.0, ALU.add, ALU.mult)
                last.then_inc(st0, 1)
                eng.wait_ge(st0, 1)
                eng.tensor_copy(flat(state_h[0]), state[:]).then_inc(st0, 1)
                eng.wait_ge(st0, 2)
                eng.tensor_tensor(flat(state_h[1]), state[:], flat(state_h[0]), ALU.subtract).then_inc(setup_ok, 1)

            for t in (*qd, *pd, *vn, biasw, zero):
                v = t[:].rearrange("p a b c -> p (a b c)") if len(t.shape) == 4 else (
                    flat(t) if len(t.shape) == 3 else t[:])
                eng.memset(v.bitcast(F32), 0.0).then_inc(zeroed, 1)
            eng.wait_ge(zeroed, 8)
            eng.memset(vn[0][:, :, HD:HD + 1], SW / SA)
            eng.memset(ones[:], 1.0).then_inc(zeroed, 1)
            eng.wait_ge(ld_small, 96)
            weights_lo(tok_st, tokw, SW, 1)
            before = {-1: lambda: weights_lo(qkv_st, qkvw, SW, 2), 0: rest_lo}
            iterate(eng, body, before)
            eng.wait_ge(st_ok[1], PAIRS)
            for n in range(2):
                eng.tensor_copy(state_d[n][:], state_h[n][:].unsqueeze(2).broadcast_to([P, KD, 2, TOKENS])
                                ).then_inc(dup_ok, 1)
            eng.wait_ge(cu_done, 1)
            eng.scalar_tensor_tensor(out=cub[:], in0=p_a[:, 0:DIM], scalar=1 / SW, in1=ffnbo[:],
                                     op0=ALU.mult, op1=ALU.add).then_inc(cub_ok, 1)
            eng.wait_ge(cub_ok, 1)
            eng.wait_ge(xo_ok, PAIRS)

            def add_state(n):
                if n >= 2:
                    eng.wait_ge(stored[n % 2], 16 * (n // 2))
                eng.tensor_tensor(fin[:, n % 2, :].rearrange("p (a d) -> p a d", a=4), xo_all[:, 4 * n:4 * n + 4, :],
                                  cub[:].unsqueeze(1).broadcast_to([P, 4, DIM]), ALU.add).then_inc(fin_in, 1)

            add_state(0)
            for n in range(PAIRS // 4):
                if n + 1 < PAIRS // 4:
                    add_state(n + 1)
                eng.wait_ge(fin_tanh, n + 1)
                eng.tensor_tensor(fin[:, n % 2, :].rearrange("p (a d) -> p a d", a=4),
                                  fin_t[:, n % 2, :].rearrange("p (a d) -> p a d", a=4),
                                  h_all[:, 4 * n:4 * n + 4, :], ALU.add).then_inc(fin_ok, 1)


def kernel(**inputs):
    import numpy as np
    import concourse.bacc as bacc
    from concourse import mybir as mb
    from concourse.bass_utils import run_bass_kernel_spmd

    a = {k: np.asarray(v) for k, v in inputs.items()}

    def rows(w):
        o, k = w.shape
        return np.ascontiguousarray(w.T.reshape(k // P, P, o).transpose(1, 0, 2).reshape(P, -1))

    x = a["x"].reshape(PAIRS, 2, 3, 8, 16, 8, 16).transpose(0, 2, 4, 6, 1, 3, 5)
    x = x.reshape(PAIRS, XC, P, P).transpose(0, 2, 1, 3).reshape(PAIRS, P, XC * P)
    arrays = {
        "in_x": np.ascontiguousarray(x),
        "in_tok_w": rows(a["L0_tok_W"]),
        "in_tok_b": a["L0_tok_b"],
        "in_qkv_w": rows(a["L0_attn_W_qkv"]),
        "in_out_w": rows(a["L0_attn_W_out"]),
        "in_out_b": a["L0_attn_b_out"],
        "in_ffn_w": rows(np.concatenate([a[f"L0_ffn_w{g}"] for g in "fico"])),
        "in_rec_w": rows(np.concatenate([a[f"L0_ffn_u{g}"] for g in "fico"])),
        "in_gate_b": np.concatenate([a[f"L0_ffn_b{g}"] for g in "fic"]).reshape(1, GATES),
        "in_ffn_bo": a["L0_ffn_bo"],
        "in_c": np.ascontiguousarray(a["L0_ffn_in_c"].reshape(KD, P).T),
    }
    nc = bacc.Bacc("TRN2", target_bir_lowering=False, num_devices=1)
    args = [nc.dram_tensor(n, v.shape, mb.dt.from_np(v.dtype), kind="ExternalInput").ap() for n, v in arrays.items()]
    args.append(nc.dram_tensor("out_h", (PAIRS, P, DIM), mb.dt.float32, kind="ExternalOutput").ap())
    build_program(nc, *args)
    r = run_bass_kernel_spmd(nc, [arrays], core_ids=[0])
    return r.results[0]["out_h"].reshape(IMAGES, TOKENS, DIM)
```

```python
import math
from contextlib import ExitStack

import concourse.bass as bass
from concourse import mybir

F32 = mybir.dt.float32
F16 = mybir.dt.float16
I32 = mybir.dt.int32
ALU = mybir.AluOpType
ACT = mybir.ActivationFunctionType

P = 128
IMAGES, TOKENS, DIM = 64, 64, 256
PAIRS = IMAGES // 2
PATCH = 3 * 16 * 16
XC = PATCH // P
HEADS, HD = 16, 64
INNER = HEADS * HD
HP = HEADS // 2
KD = DIM // P
GATES = 3 * DIM
GM = GATES // P
TOPK = max(1, int(0.1 * TOKENS))
EPS = 1e-5
NEWTON = 3
RSQRT_BITS = float(0x5F3759DF)
VW = HD + 2

SW = 64.0
SQ = 4.0
SE = DIM ** -0.5 / (SQ * SQ)
SA = 4.0
SP = 256.0
SU = SW / 2

FIN = 8
FP = PAIRS // FIN
FIN_POOL = (1, 4)

FIRST, LAST = -2, PAIRS + 1
LOOP_FROM, LOOP_TO = 3, PAIRS - 2

FILLS = ("k1", "k0", "q1", "q0", "v0", "v1")
WEIGHTS = ("tok0", "tok1", *FILLS, "out", "ffn", "rec")


def count(name):
    return WEIGHTS.index(name) + 1


def column(name):
    return INNER * "qkv".index(name[0]) + 512 * int(name[1])


def build_program(nc, x, tok_w, tok_b, qkv_w, out_w, out_b, ffn_w, rec_w, gate_b, ffn_bo, in_c, out):
    with ExitStack() as ctx:
        def sb(name, shape, dt):
            return ctx.enter_context(nc.sbuf_tensor(name, shape, dt))

        def bank(name):
            return ctx.enter_context(nc.psum_tensor(name, [P, 512], F32))

        def sem(name):
            return ctx.enter_context(nc.semaphore(name))

        tokw = [sb(f"tokw_{s}", [P, XC, DIM], F16) for s in ("hi", "lo")]
        qkvw = [sb(f"qkvw_{s}", [P, KD, 3 * INNER], F16) for s in ("hi", "lo")]
        outw = [sb(f"outw_{s}", [P, HP, DIM], F16) for s in ("hi", "lo")]
        ffnw = [sb(f"ffnw_{s}", [P, KD, 4 * DIM], F16) for s in ("hi", "lo")]
        recw = [sb(f"recw_{s}", [P, KD, 4 * DIM], F16) for s in ("hi", "lo")]
        gateb = sb("gateb", [P, GM], F32)
        tokb = sb("tokb", [P, DIM], F32)
        outb = sb("outb", [P, DIM], F32)
        ffnbo = sb("ffnbo", [P, DIM], F32)
        c0 = sb("c0", [P, KD], F32)
        ident = sb("ident", [P, P], F32)
        h_all = sb("h_all", [P, PAIRS, DIM], F32)
        xo_all = sb("xo_all", [P, PAIRS, DIM], F32)
        xo_flat = xo_all[:, :, :].rearrange("p a d -> p (a d)")
        h_flat = h_all[:, :, :].rearrange("p a d -> p (a d)")
        tok_st = xo_flat[:, 0:XC * DIM].rearrange("p (c d) -> p c d", d=DIM)
        qkv_st = xo_flat[:, XC * DIM:XC * DIM + KD * 3 * INNER].rearrange("p (c d) -> p c d", d=3 * INNER)
        tail = 8 * DIM
        out_st = h_flat[:, tail:tail + HP * DIM].rearrange("p (c d) -> p c d", d=DIM)
        ffn_st = h_flat[:, tail + HP * DIM:tail + HP * DIM + KD * 4 * DIM].rearrange("p (c d) -> p c d", d=4 * DIM)
        rec_st = h_flat[:, tail + HP * DIM + KD * 4 * DIM:tail + HP * DIM + 2 * KD * 4 * DIM].rearrange(
            "p (c d) -> p c d", d=4 * DIM)
        half = XC // 2
        split = {f"tok{n}": (tok_st[:, n * half:(n + 1) * half, :],
                             [t[:, n * half:(n + 1) * half, :] for t in tokw], SW) for n in range(2)}
        split.update({n: (qkv_st[:, :, column(n):column(n) + 512],
                          [t[:, :, column(n):column(n) + 512] for t in qkvw], SW) for n in FILLS})
        split.update(out=(out_st, [t[:] for t in outw], SW), ffn=(ffn_st, [t[:] for t in ffnw], SW),
                     rec=(rec_st, [t[:] for t in recw], SU))
        xf = sb("xf", [P, XC * P], F32)
        xs = [sb(f"xs_{s}", [P, XC, P], F16) for s in ("hi", "lo")]
        z1 = sb("z1", [P, DIM], F32)
        z2 = sb("z2", [P, DIM], F32)
        st1 = sb("st1", [P, 6], F32)
        st2 = sb("st2", [P, 6], F32)
        mv1 = sb("mv1", [P, 2], F32)
        mv2 = sb("mv2", [P, 2], F32)
        rs1 = sb("rs1", [P, 1], F32)
        rs2 = sb("rs2", [P, 1], F32)
        nt = sb("nt", [P, 1], F32)
        z1t = [sb(f"z1t_{s}", [P, KD, P], F16) for s in ("hi", "lo")]
        z2t = [sb(f"z2t_{s}", [P, KD, P], F16) for s in ("hi", "lo")]
        qd = [sb(f"qd_{s}", [P, HP, 2, P], F16) for s in ("hi", "lo")]
        kt = [sb(f"kt_{s}", [P, HP, P], F16) for s in ("hi", "lo")]
        vn = [sb(f"vn_{s}", [P, HEADS, VW], F16) for s in ("hi", "lo")]
        top8 = [sb(f"top8_{n}", [P, 8, 8], F32) for n in range(2)]
        ebias = [sb(f"ebias_{n}", [P, 8], F32) for n in range(2)]
        keep = [sb(f"keep_{n}", [P, 512], F16) for n in range(2)]
        expo = [sb(f"expo_{n}", [P, 512], F32) for n in range(2)]
        wts = [sb(f"wts_{n}", [P, 512], F32) for n in range(2)]
        pd = [sb(f"pd_{s}", [P, 8, P], F16) for s in ("hi", "lo")]
        rden = sb("rden", [P, 4], F32)
        att = sb("att", [P, HEADS, HD], F32)
        att_t = [sb(f"att_t_{s}", [P, HP, P], F16) for s in ("hi", "lo")]
        tfi = sb("tfi", [P, 2 * P], F32)
        tg = sb("tg", [P, P], F32)
        fs = sb("fs", [P, P], F32)
        ig = sb("ig", [P, P], F32)
        state = sb("state", [P, KD * TOKENS], F32)
        state_h = [sb(f"state_{s}", [P, KD, TOKENS], F16) for s in ("hi", "lo")]
        state_d = [sb(f"state_d_{s}", [P, KD, 2, TOKENS], F16) for s in ("hi", "lo")]
        cub = sb("cub", [P, DIM], F32)
        zero = sb("zero", [P, TOKENS], F32)

        p_gate = [bank("p_gate0"), bank("p_gate1")]
        p_a, p_b = bank("p_a"), bank("p_b")
        p_s = [bank("p_s0"), bank("p_s1")]
        p_t = bank("p_t")
        p_av = bank("p_av")

        ld = {n: sem(f"ld_{n}") for n in WEIGHTS}
        ld_small = sem("ld_small")
        ld_x = sem("ld_x")
        passed = sem("passed")
        made = sem("made")
        zeroed = sem("zeroed")
        bias_ok = sem("bias_ok")
        ident_ok = sem("ident_ok")
        wh = sem("wh")
        wl = sem("wl")
        setup_ok = sem("setup_ok")
        x_hi, x_lo = sem("x_hi"), sem("x_lo")
        tok_done, h1_ok, ln1, z1_ok = sem("tok_done"), sem("h1_ok"), sem("ln1"), sem("z1_ok")
        rstd1, rstd2 = sem("rstd1"), sem("rstd2")
        res_ok = sem("res_ok")
        z1t_done, z1t_hi, z1t_lo = sem("z1t_done"), sem("z1t_hi"), sem("z1t_lo")
        f_done = {n: sem(f"{n}_done") for n in FILLS}
        f_hi = {n: sem(f"{n}_hi") for n in FILLS}
        f_lo = {n: sem(f"{n}_lo") for n in FILLS}
        s_done = [sem(f"s_done{n}") for n in range(2)]
        max_ok = [sem(f"max_ok{n}") for n in range(2)]
        ebias_ok = [sem(f"ebias_ok{n}") for n in range(2)]
        keep_ok = [sem(f"keep_ok{n}") for n in range(2)]
        exp_ok = [sem(f"exp_ok{n}") for n in range(2)]
        wts_ok = [sem(f"wts_ok{n}") for n in range(2)]
        pt_done = [sem(f"pt_done{n}") for n in range(2)]
        pt_hi = [sem(f"pt_hi{n}") for n in range(2)]
        pt_lo = [sem(f"pt_lo{n}") for n in range(2)]
        av_done = [sem(f"av_done{n}") for n in range(4)]
        rden_ok = [sem(f"rden_ok{n}") for n in range(4)]
        att_ok = [sem(f"att_ok{n}") for n in range(4)]
        at_done = [sem(f"at_done{n}") for n in range(2)]
        at_hi = [sem(f"at_hi{n}") for n in range(2)]
        at_lo = [sem(f"at_lo{n}") for n in range(2)]
        y_done, h2_ok, ln2, z2_ok = sem("y_done"), sem("h2_ok"), sem("ln2"), sem("z2_ok")
        z2t_done, z2t_hi, z2t_lo = sem("z2t_done"), sem("z2t_hi"), sem("z2t_lo")
        gx_done, xo_done, xo_ok = sem("gx_done"), sem("xo_done"), sem("xo_ok")
        rec_done = [sem(f"rec_done{n}") for n in range(2)]
        gate_ok = [sem(f"gate_ok{n}") for n in range(2)]
        rec_step = [sem(f"rec_step{n}") for n in range(2)]
        st_ok = [sem(f"st_ok{n}") for n in range(2)]
        st0 = sem("st0")
        dup_ok, cu_done, cub_ok = sem("dup_ok"), sem("cu_done"), sem("cub_ok")
        fin_in, fin_tanh, stored = sem("fin_in"), sem("fin_tanh"), sem("stored")
        fin_ok = [sem(f"fin_ok{n}") for n in range(FIN)]

        def first(i, at):
            return isinstance(i, int) and i == at

        def valid(p):
            return not isinstance(p, int) or 0 <= p < PAIRS

        turns_a = [(f_lo["k1"], 1), (f_lo["q1"], 1), (f_lo["q0"], 1), (f_lo["v1"], 1)]
        turns_b = [(h2_ok, -1), (f_lo["k0"], 1), (h1_ok, 2), (f_lo["v0"], 1), (xo_ok, -1)]
        turns_t = [(z1t_lo, 1), (pt_lo[0], 0), (z2t_lo, -1), (pt_lo[1], 0), (at_lo[0], 0), (at_lo[1], 0)]
        turns_v = [(att_ok[0], 0), (att_ok[1], 0), (att_ok[2], 0), (att_ok[3], 0)]
        home = {n: (p_a, turns_a) for n in ("k1", "q1", "q0", "v1")}
        home.update({n: (p_b, turns_b) for n in ("project", "k0", "embed", "v0", "out_x")})

        def bank_free(eng, turns, reader, i):
            at = [t[0] is reader for t in turns].index(True)
            n = i
            while True:
                at -= 1
                if at < 0:
                    at, n = len(turns) - 1, n - 1
                if isinstance(n, int) and n < FIRST:
                    return
                s, lag = turns[at]
                if valid(n + lag):
                    eng.wait_ge(s, n + lag + 1)
                    return

        def wait_alone(eng, s, value):
            eng.wait_ge(s, value)
            eng.sem_inc(passed, 1)

        def iterate(eng, body):
            for i in range(FIRST, LOOP_FROM):
                body(i)
            with eng.Fori(LOOP_FROM, LOOP_TO) as i:
                body(i)
            for i in range(LOOP_TO, LAST + 1):
                body(i)

        block = ctx.enter_context(nc.Block())

        @block.sync
        def _(eng):
            eng.dma_start(xf[:], x[0]).then_inc(ld_x, 16)
            for n in range(2):
                eng.dma_start(split[f"tok{n}"][0], tok_w[:, n * half:(n + 1) * half, :]).then_inc(ld[f"tok{n}"], 16)
            eng.dma_start(tokb[:], tok_b.partition_broadcast(P)).then_inc(ld_small, 16)
            eng.dma_start(outb[:], out_b.partition_broadcast(P)).then_inc(ld_small, 16)
            eng.dma_start(ffnbo[:], ffn_bo.partition_broadcast(P)).then_inc(ld_small, 16)
            eng.dma_start(c0[:], in_c).then_inc(ld_small, 16)
            eng.dma_start(gateb[:], gate_b).then_inc(ld_small, 16)
            for n in FILLS:
                eng.dma_start(split[n][0], qkv_w[:, :, column(n):column(n) + 512]).then_inc(ld[n], 16)

            def patches(p):
                eng.wait_ge(x_hi, p)
                eng.wait_ge(x_lo, p)
                eng.dma_start(xf[:], x[p]).then_inc(ld_x, 16)

            patches(1)
            eng.dma_start(out_st, out_w).then_inc(ld["out"], 16)
            eng.dma_start(ffn_st, ffn_w).then_inc(ld["ffn"], 16)
            eng.dma_start(rec_st, rec_w).then_inc(ld["rec"], 16)
            with eng.Fori(2, PAIRS) as p:
                patches(p)
            for n in range(FIN):
                eng.wait_ge(fin_ok[n], 1)
                eng.dma_start(out[FP * n:FP * n + FP].rearrange("a p d -> p a d"),
                              h_all[:, FP * n:FP * n + FP, :]).then_inc(stored, 16)
            eng.wait_ge(stored, 16 * FIN)

        @block.gpsimd
        def _(eng):
            eng.memset(ident[:], 0.0).then_inc(made, 1)
            eng.wait_ge(made, 1)
            eng.affine_select(out=ident[:], in_=ident[:], compare_op=ALU.not_equal, fill=1.0, base=0,
                              pattern=[[-1, P]], channel_multiplier=1).then_inc(ident_ok, 1)
            eng.wait_ge(ld_small, 80)
            eng.tensor_scalar(gateb[:, 0:4], gateb[:, 0:4], 0.5, None, ALU.mult).then_inc(bias_ok, 1)

            def patches_lo(i):
                eng.wait_ge(x_hi, i + 3)
                eng.tensor_tensor(xs[1][:].rearrange("p c t -> p (c t)"), xf[:],
                                  xs[0][:].rearrange("p c t -> p (c t)"), ALU.subtract).then_inc(x_lo, 1)

            def add_bias(i):
                eng.wait_ge(z1_ok, i + 3)
                eng.tensor_tensor(h_all[:, i + 2, :], h_all[:, i + 2, :], outb[:], ALU.add).then_inc(res_ok, 1)

            def exp_bias(i, hf):
                wait_alone(eng, max_ok[hf], i + 1)
                eng.tensor_scalar(ebias[hf][:], top8[hf][:, :, 0], -SE, None, ALU.mult).then_inc(ebias_ok[hf], 1)

            def inverse_deviation(p, mv, rs, chain, ok):
                var, y, t = mv[:, 1:2], rs[:], nt[:]
                at = 3 * NEWTON * p
                wait_alone(eng, chain, 4 * p + 4)
                for n in range(NEWTON):
                    if n:
                        wait_alone(eng, ok, at + 3 * n)
                    eng.tensor_scalar(t, y, y, var, ALU.mult, ALU.mult).then_inc(ok, 1)
                    wait_alone(eng, ok, at + 3 * n + 1)
                    eng.tensor_scalar(t, t, -0.5, 1.5, ALU.mult, ALU.add).then_inc(ok, 1)
                    wait_alone(eng, ok, at + 3 * n + 2)
                    eng.tensor_tensor(y, y, t, ALU.mult).then_inc(ok, 1)

            def mask(i, hf):
                eng.wait_ge(exp_ok[hf], i + 1)
                eng.wait_ge(keep_ok[hf], i + 1)
                eng.tensor_tensor(wts[hf][:], expo[hf][:], keep[hf][:], ALU.mult).then_inc(wts_ok[hf], 1)

            def body(i):
                if valid(i):
                    exp_bias(i, 0)
                if valid(i + 2):
                    patches_lo(i)
                if valid(i):
                    mask(i, 0)
                    exp_bias(i, 1)
                if valid(i - 1):
                    inverse_deviation(i - 1, mv2, rs2, ln2, rstd2)
                if valid(i):
                    mask(i, 1)
                if valid(i + 2):
                    inverse_deviation(i + 2, mv1, rs1, ln1, rstd1)
                    add_bias(i)
            iterate(eng, body)
            for n in FIN_POOL:
                eng.wait_ge(fin_tanh, n + 1)
                eng.tensor_tensor(h_all[:, FP * n:FP * n + FP, :], xo_all[:, FP * n:FP * n + FP, :],
                                  h_all[:, FP * n:FP * n + FP, :], ALU.add).then_inc(fin_ok[n], 1)

        @block.tensor
        def _(eng):
            def mm3(o, stat, mov, start, stop, skip=False):
                sh, sl = stat
                mh, ml = mov
                eng.matmul(o, sh, mh, start=start, stop=False, skip_group_check=skip)
                eng.matmul(o, sh, ml, start=False, stop=False, skip_group_check=skip)
                return eng.matmul(o, sl, mh, start=False, stop=stop, skip_group_check=skip)

            def part(pair, f):
                return [f(t) for t in pair]

            def embed(i):
                p = i + 2
                eng.wait_ge(x_hi, p + 1)
                eng.wait_ge(x_lo, p + 1)
                bank_free(eng, home["embed"][1], h1_ok, i)
                for c in range(XC):
                    if first(i, FIRST) and c % half == 0:
                        eng.wait_ge(wl, count(f"tok{c // half}"))
                    last = mm3(home["embed"][0][:, 0:DIM], part(xs, lambda t: t[:, c, :]), part(tokw, lambda t: t[:, c, :]),
                               c == 0, c == XC - 1)
                last.then_inc(tok_done, 1)

            def turn_z(i, z, ready, turns, reader, done, p):
                eng.wait_ge(ready, p + 1)
                bank_free(eng, turns, reader, i)
                for k in range(KD):
                    last = eng.transpose(p_t[:, k * P:(k + 1) * P], z[:, k * P:(k + 1) * P], ident[:])
                last.then_inc(done, 1)

            def fill(i, name):
                p = i + 1
                bnk, turns = home[name]
                if name == FILLS[0]:
                    eng.wait_ge(z1t_lo, p + 1)
                bank_free(eng, turns, f_lo[name], i)
                if first(p, 0):
                    eng.wait_ge(wl, count(name))
                o = column(name)
                if name[0] == "v":
                    for k in range(KD):
                        last = mm3(bnk[:, :], part(z1t, lambda t: t[:, k, :]),
                                   part(qkvw, lambda t: t[:, k, o:o + 512]), k == 0, k == KD - 1)
                else:
                    for c in range(4):
                        for k in range(KD):
                            last = mm3(bnk[:, c * P:(c + 1) * P],
                                       part(qkvw, lambda t: t[:, k, o + c * P:o + (c + 1) * P]),
                                       part(z1t, lambda t: t[:, k, :]), k == 0, k == KD - 1)
                last.then_inc(f_done[name], 1)

            def scores(i, hf):
                eng.wait_ge(f_lo[f"q{hf}"], i + 1)
                eng.wait_ge(f_lo[f"k{hf}"], i + 1)
                if not isinstance(i, int) or i > 0:
                    eng.wait_ge(exp_ok[hf], i)
                for c in range(4):
                    for m in range(2):
                        last = mm3(p_s[hf][:, (2 * c + m) * 64:(2 * c + m + 1) * 64],
                                   part(qd, lambda t: t[:, 4 * hf + c, m, :]),
                                   part(kt, lambda t: t[:, 4 * hf + c, 64 * m:64 * m + 64]), True, True)
                last.then_inc(s_done[hf], 1)

            def turn_weights(i, hf):
                eng.wait_ge(wts_ok[hf], i + 1)
                bank_free(eng, turns_t, pt_lo[hf], i)
                for c in range(4):
                    last = eng.transpose(p_t[:, c * P:(c + 1) * P], wts[hf][:, c * P:(c + 1) * P], ident[:])
                last.then_inc(pt_done[hf], 1)

            def attend(i, qr):
                hf = qr // 2
                eng.wait_ge(pt_lo[hf], i + 1)
                eng.wait_ge(f_lo[f"v{hf}"], i + 1)
                bank_free(eng, turns_v, att_ok[qr], i)
                for n in range(4):
                    head = 4 * qr + n
                    last = mm3(p_av[:, n * VW:(n + 1) * VW], part(pd, lambda t: t[:, head % 8, :]),
                               part(vn, lambda t: t[:, head, :]), True, True)
                last.then_inc(av_done[qr], 1)

            def turn_att(i, hf):
                eng.wait_ge(att_ok[2 * hf + 1], i + 1)
                bank_free(eng, turns_t, at_lo[hf], i)
                for c in range(4):
                    j = 4 * hf + c
                    last = eng.transpose(p_t[:, c * P:(c + 1) * P],
                                         att[:, 2 * j:2 * j + 2, :].rearrange("p h d -> p (h d)"), ident[:])
                last.then_inc(at_done[hf], 1)

            def project(i):
                p = i - 1
                eng.wait_ge(at_lo[0], p + 1)
                eng.wait_ge(at_lo[1], p + 1)
                bank_free(eng, home["project"][1], h2_ok, i)
                if first(p, 0):
                    eng.wait_ge(wl, count("out"))
                for j in range(HP):
                    last = mm3(home["project"][0][:, 0:DIM], part(att_t, lambda t: t[:, j, :]),
                               part(outw, lambda t: t[:, j, :]), j == 0, j == HP - 1)
                last.then_inc(y_done, 1)

            def gates_x(i):
                p = i - 1
                eng.wait_ge(z2t_lo, p + 1)
                if not isinstance(p, int) or p > 0:
                    for s in range(2):
                        eng.wait_ge(gate_ok[s], GM * p)
                if first(p, 0):
                    eng.wait_ge(wl, count("ffn"))
                for m in range(GM):
                    for k in range(KD):
                        for wgt, zz in ((0, 0), (0, 1), (1, 0)):
                            for s in range(2):
                                last = eng.matmul(p_gate[s][:, m * 64:m * 64 + 64],
                                                  ffnw[wgt][:, k, m * P:(m + 1) * P],
                                                  z2t[zz][:, k, 64 * s:64 * s + 64],
                                                  start=(m == 0 and k == 0 and wgt == zz == 0), stop=False,
                                                  skip_group_check=True)
                last.then_inc(gx_done, 1)

            def out_x(i):
                bank_free(eng, home["out_x"][1], xo_ok, i)
                for k in range(KD):
                    last = mm3(home["out_x"][0][:, 0:DIM], part(z2t, lambda t: t[:, k, :]),
                               part(ffnw, lambda t: t[:, k, GATES:GATES + DIM]), k == 0, k == KD - 1)
                last.then_inc(xo_done, 1)

            def recur(p, s):
                if s == 1:
                    eng.wait_ge(st_ok[0], p + 1)
                elif isinstance(p, int) and p == 0:
                    eng.wait_ge(setup_ok, 1)
                    eng.wait_ge(wl, count("rec"))
                else:
                    eng.wait_ge(st_ok[1], p)
                for m in range(GM):
                    for k in range(KD):
                        last = mm3(p_gate[s][:, m * 64:m * 64 + 64],
                                   part(recw, lambda t: t[:, k, m * P:(m + 1) * P]),
                                   part(state_h, lambda t: t[:, k, :]), False, m == GM - 1 and k == KD - 1, True)
                last.then_inc(rec_done[s], 1)

            def body(i):
                if valid(i):
                    scores(i, 0)
                if valid(i + 1):
                    turn_z(i, z1, z1_ok, turns_t, z1t_lo, z1t_done, i + 1)
                if valid(i - 1):
                    project(i)
                if valid(i):
                    scores(i, 1)
                if valid(i + 1):
                    fill(i, "k1")
                    fill(i, "k0")
                if valid(i):
                    turn_weights(i, 0)
                if valid(i + 1):
                    fill(i, "q1")
                if valid(i + 2):
                    embed(i)
                if valid(i - 2):
                    recur(i - 2, 1)
                if valid(i):
                    attend(i, 0)
                if valid(i - 1):
                    turn_z(i, z2, z2_ok, turns_t, z2t_lo, z2t_done, i - 1)
                if valid(i + 1):
                    fill(i, "q0")
                if valid(i):
                    attend(i, 1)
                    turn_weights(i, 1)
                if valid(i - 1):
                    gates_x(i)
                if valid(i + 1):
                    fill(i, "v0")
                if valid(i):
                    attend(i, 2)
                    turn_att(i, 0)
                if valid(i - 1):
                    recur(i - 1, 0)
                if valid(i):
                    attend(i, 3)
                if valid(i + 1):
                    fill(i, "v1")
                if valid(i):
                    turn_att(i, 1)
                if valid(i - 1):
                    out_x(i)

            eng.wait_ge(ident_ok, 1)
            iterate(eng, body)
            eng.wait_ge(dup_ok, 2)
            for k in range(KD):
                last = mm3(p_a[:, 0:DIM], part(state_d, lambda t: t[:, k, :, :].rearrange("p a t -> p (a t)")),
                           part(recw, lambda t: t[:, k, GATES:GATES + DIM]), k == 0, k == KD - 1)
            last.then_inc(cu_done, 1)

        @block.scalar
        def _(eng):
            def weights_hi(name):
                st, pair, scale = split[name]
                eng.wait_ge(ld[name], 16)
                eng.activation(pair[0], st, ACT.Copy, scale=scale).then_inc(wh, 1)

            def flat(t):
                return t[:].rearrange("p a b -> p (a b)")

            def patches_hi(i):
                p = i + 2
                eng.wait_ge(ld_x, 16 * (p + 1))
                if not isinstance(p, int) or p > 0:
                    eng.wait_ge(tok_done, p)
                eng.activation(flat(xs[0]), xf[:], ACT.Copy).then_inc(x_hi, 1)

            def fill_hi(i, name):
                p = i + 1
                hf = int(name[1])
                src = home[name][0]
                eng.wait_ge(f_done[name], p + 1)
                if name[0] == "q":
                    for u in range(2):
                        r = slice(64 * u, 64 * u + 64)
                        last = eng.activation(
                            qd[0][r, 4 * hf:4 * hf + 4, :, r].rearrange("p c m t -> p (c m) t"),
                            src[r, :].rearrange("p (c t) -> p c t", t=64), ACT.Copy, scale=SQ / SW)
                    last.then_inc(f_hi[name], 1)
                elif name[0] == "k":
                    eng.activation(kt[0][:, 4 * hf:4 * hf + 4, :].rearrange("p c t -> p (c t)"), src[:, :],
                                   ACT.Copy, scale=SQ / SW).then_inc(f_hi[name], 1)
                else:
                    eng.activation(vn[0][:, 8 * hf:8 * hf + 8, 0:HD], src[:, :].rearrange("p (h d) -> p h d", d=HD),
                                   ACT.Relu).then_inc(f_hi[name], 1)

            def exponentials(i, hf):
                eng.wait_ge(keep_ok[hf], i + 1)
                eng.wait_ge(ebias_ok[hf], i + 1)
                for u in range(8):
                    last = eng.activation(expo[hf][:, 64 * u:64 * u + 64], p_s[hf][:, 64 * u:64 * u + 64], ACT.Exp,
                                          bias=ebias[hf][:, u:u + 1], scale=SE)
                last.then_inc(exp_ok[hf], 1)

            def weights_t_hi(i, hf):
                eng.wait_ge(pt_done[hf], i + 1)
                for u in range(2):
                    r = slice(64 * u, 64 * u + 64)
                    last = eng.activation(pd[0][r, :, r], p_t[r, :].rearrange("p (h t) -> p h t", t=64),
                                          ACT.Copy, scale=SP)
                last.then_inc(pt_hi[hf], 1)

            def att_hi(p, hf):
                eng.wait_ge(at_done[hf], p + 1)
                eng.activation(att_t[0][:, 4 * hf:4 * hf + 4, :].rearrange("p c t -> p (c t)"), p_t[:, :],
                               ACT.Copy).then_inc(at_hi[hf], 1)

            def z_hi(p, zt, done, ok):
                eng.wait_ge(done, p + 1)
                eng.activation(flat(zt[0]), p_t[:, 0:DIM], ACT.Copy).then_inc(ok, 1)

            def gate_tanh(p, s):
                eng.wait_ge(rec_done[s], p + 1)
                if s == 1:
                    eng.wait_ge(st_ok[0], p + 1)
                elif not isinstance(p, int) or p > 0:
                    eng.wait_ge(st_ok[1], p)
                if first(p, 0) and s == 0:
                    eng.wait_ge(bias_ok, 1)
                for m in range(GM):
                    o, scale = (tfi[:, 64 * m:64 * m + 64], 0.5) if m < 4 else (tg[:, 64 * m - 256:64 * m - 192], 1.0)
                    eng.activation(o, p_gate[s][:, 64 * m:64 * m + 64], ACT.Tanh, bias=gateb[:, m:m + 1],
                                   scale=scale / SW).then_inc(gate_ok[s], 1)

            def out_x_copy(i):
                eng.wait_ge(xo_done, i)
                eng.activation(xo_all[:, i - 1, :], home["out_x"][0][:, 0:DIM], ACT.Copy, scale=1 / SW).then_inc(xo_ok, 1)

            def body(i):
                if valid(i + 2) and not first(i, FIRST):
                    patches_hi(i)
                if valid(i + 1):
                    z_hi(i + 1, z1t, z1t_done, z1t_hi)
                if valid(i):
                    exponentials(i, 0)
                if valid(i + 1):
                    fill_hi(i, "k1")
                    fill_hi(i, "k0")
                if valid(i):
                    weights_t_hi(i, 0)
                if valid(i + 1):
                    fill_hi(i, "q1")
                if valid(i):
                    exponentials(i, 1)
                if first(i, 0):
                    weights_hi("out")
                if first(i, 1):
                    weights_hi("rec")
                if valid(i - 2):
                    gate_tanh(i - 2, 1)
                if valid(i - 1):
                    z_hi(i - 1, z2t, z2t_done, z2t_hi)
                if valid(i):
                    weights_t_hi(i, 1)
                if valid(i + 1):
                    fill_hi(i, "q0")
                    fill_hi(i, "v0")
                if valid(i):
                    att_hi(i, 0)
                if first(i, 0):
                    weights_hi("ffn")
                if valid(i - 1):
                    gate_tanh(i - 1, 0)
                if valid(i):
                    att_hi(i, 1)
                if valid(i + 1):
                    fill_hi(i, "v1")
                if valid(i - 1):
                    out_x_copy(i)

            patches_hi(FIRST)
            for n in ("tok0", "tok1", *FILLS):
                weights_hi(n)
            eng.wait_ge(zeroed, 7)
            iterate(eng, body)
            for n in range(FIN):
                eng.wait_ge(fin_in, n + 1)
                eng.activation(xo_all[:, FP * n:FP * n + FP, :], xo_all[:, FP * n:FP * n + FP, :],
                               ACT.Tanh).then_inc(fin_tanh, 1)

        @block.vector
        def _(eng):
            def flat(t):
                return t[:].rearrange("p a b -> p (a b)")

            def lo(o, src, scale, hi, op=ALU.mult):
                return eng.scalar_tensor_tensor(out=o, in0=src, scalar=scale, in1=hi, op0=op, op1=ALU.subtract)

            def weights_lo(name):
                st, pair, scale = split[name]
                eng.wait_ge(wh, count(name))
                lo(pair[1], st, scale, pair[0]).then_inc(wl, 1)

            def start_state():
                for k in range(KD):
                    last = eng.tensor_scalar(state[:, k * TOKENS:(k + 1) * TOKENS], zero[:, 0:TOKENS],
                                             c0[:, k:k + 1], 2.0, ALU.add, ALU.mult)
                last.then_inc(st0, 1)
                eng.wait_ge(st0, 1)
                eng.tensor_copy(flat(state_h[0]), state[:]).then_inc(st0, 1)
                eng.wait_ge(st0, 2)
                eng.tensor_tensor(flat(state_h[1]), state[:], flat(state_h[0]), ALU.subtract).then_inc(setup_ok, 1)

            def statistics(p, h_ok, h, st, mv, rs, chain):
                wait_alone(eng, h_ok, p + 1)
                eng.bn_stats(st[:], h).then_inc(chain, 1)
                wait_alone(eng, chain, 4 * p + 1)
                eng.bn_aggr(mv[:], st[:]).then_inc(chain, 1)
                eng.wait_ge(chain, 4 * p + 2)
                eng.tensor_scalar(mv[:, 1:2], mv[:, 1:2], EPS, None, ALU.add).then_inc(chain, 1)
                eng.wait_ge(chain, 4 * p + 3)
                eng.tensor_scalar(rs[:].bitcast(I32), mv[:, 1:2].bitcast(I32), -0.5, RSQRT_BITS,
                                  ALU.mult, ALU.add).then_inc(chain, 1)

            def normal(p, mv, rs, z, rstd, z_ok):
                eng.wait_ge(rstd, 3 * NEWTON * (p + 1))
                eng.tensor_scalar(z[:], h_all[:, p, :], mv[:, 0:1], rs[:], ALU.subtract, ALU.mult).then_inc(z_ok, 1)

            def embed_out(i):
                p = i + 2
                eng.wait_ge(tok_done, p + 1)
                eng.scalar_tensor_tensor(out=h_all[:, p, :], in0=home["embed"][0][:, 0:DIM], scalar=1 / SW, in1=tokb[:],
                                         op0=ALU.mult, op1=ALU.add).then_inc(h1_ok, 1)
                statistics(p, h1_ok, h_all[:, p, :], st1, mv1, rs1, ln1)

            def project_out(i):
                p = i - 1
                eng.wait_ge(y_done, p + 1)
                eng.wait_ge(res_ok, p + 1)
                eng.scalar_tensor_tensor(out=h_all[:, p, :], in0=home["project"][0][:, 0:DIM], scalar=1 / (SW * SA),
                                         in1=h_all[:, p, :], op0=ALU.mult, op1=ALU.add).then_inc(h2_ok, 1)
                statistics(p, h2_ok, h_all[:, p, :], st2, mv2, rs2, ln2)

            def z_lo(p, zt, hi_ok, ok):
                eng.wait_ge(hi_ok, p + 1)
                eng.tensor_tensor(flat(zt[1]), p_t[:, 0:DIM], flat(zt[0]), ALU.subtract).then_inc(ok, 1)

            def fill_lo(i, name):
                p = i + 1
                hf = int(name[1])
                src = home[name][0]
                eng.wait_ge(f_hi[name], p + 1)
                if name[0] == "q":
                    for u in range(2):
                        r = slice(64 * u, 64 * u + 64)
                        o, hi = (t[r, 4 * hf:4 * hf + 4, :, r].rearrange("p c m t -> p (c m) t")
                                 for t in (qd[1], qd[0]))
                        last = lo(o, src[r, :].rearrange("p (c t) -> p c t", t=64), SQ / SW, hi)
                    last.then_inc(f_lo[name], 1)
                elif name[0] == "k":
                    o, hi = (t[:, 4 * hf:4 * hf + 4, :].rearrange("p c t -> p (c t)") for t in (kt[1], kt[0]))
                    lo(o, src[:, :], SQ / SW, hi).then_inc(f_lo[name], 1)
                else:
                    o, hi = (t[:, 8 * hf:8 * hf + 8, 0:HD] for t in (vn[1], vn[0]))
                    lo(o, src[:, :].rearrange("p (h d) -> p h d", d=HD), 0.0, hi, ALU.max).then_inc(f_lo[name], 1)

            def largest(i, hf):
                wait_alone(eng, s_done[hf], i + 1)
                for u in range(8):
                    last = eng.max(top8[hf][:, u, :], p_s[hf][:, 64 * u:64 * u + 64])
                last.then_inc(max_ok[hf], 1)

            def select(i, hf):
                eng.wait_ge(max_ok[hf], i + 1)
                eng.tensor_tensor(keep[hf][:].rearrange("p (u k) -> p u k", u=8),
                                  p_s[hf][:, :].rearrange("p (u k) -> p u k", u=8),
                                  top8[hf][:, :, TOPK - 1:TOPK].broadcast_to([P, 8, 64]),
                                  ALU.is_ge).then_inc(keep_ok[hf], 1)

            def weights_t_lo(i, hf):
                eng.wait_ge(pt_hi[hf], i + 1)
                for u in range(2):
                    r = slice(64 * u, 64 * u + 64)
                    last = lo(pd[1][r, :, r], p_t[r, :].rearrange("p (h t) -> p h t", t=64), SP, pd[0][r, :, r])
                last.then_inc(pt_lo[hf], 1)

            def normalise(i, qr):
                eng.wait_ge(av_done[qr], i + 1)
                av = p_av[:, 0:4 * VW].rearrange("p (h w) -> p h w", w=VW)
                eng.reciprocal(rden[:], av[:, :, HD]).then_inc(rden_ok[qr], 1)
                eng.wait_ge(rden_ok[qr], i + 1)
                eng.tensor_tensor(att[:, 4 * qr:4 * qr + 4, :], av[:, :, 0:HD],
                                  rden[:].unsqueeze(2).broadcast_to([P, 4, HD]), ALU.mult).then_inc(att_ok[qr], 1)

            def att_lo(p, hf):
                eng.wait_ge(at_hi[hf], p + 1)
                o, hi = (t[:, 4 * hf:4 * hf + 4, :].rearrange("p c t -> p (c t)") for t in (att_t[1], att_t[0]))
                eng.tensor_tensor(o, p_t[:, :], hi, ALU.subtract).then_inc(at_lo[hf], 1)

            def update(p, s):
                eng.wait_ge(gate_ok[s], GM * p + 2)
                eng.scalar_tensor_tensor(out=fs[:], in0=tfi[:, 0:P], scalar=1.0, in1=state[:],
                                         op0=ALU.add, op1=ALU.mult).then_inc(rec_step[s], 1)
                eng.wait_ge(gate_ok[s], GM * p + GM)
                eng.scalar_tensor_tensor(out=ig[:], in0=tfi[:, P:2 * P], scalar=1.0, in1=tg[:],
                                         op0=ALU.add, op1=ALU.mult).then_inc(rec_step[s], 1)
                eng.wait_ge(rec_step[s], 4 * p + 2)
                eng.scalar_tensor_tensor(out=state[:], in0=fs[:], scalar=0.5, in1=ig[:],
                                         op0=ALU.mult, op1=ALU.add).then_inc(rec_step[s], 1)
                eng.wait_ge(rec_step[s], 4 * p + 3)
                eng.tensor_copy(flat(state_h[0]), state[:]).then_inc(rec_step[s], 1)
                eng.wait_ge(rec_step[s], 4 * p + 4)
                eng.tensor_tensor(flat(state_h[1]), state[:], flat(state_h[0]), ALU.subtract).then_inc(st_ok[s], 1)

            def body(i):
                if valid(i):
                    largest(i, 0)
                    select(i, 0)
                if valid(i + 1):
                    z_lo(i + 1, z1t, z1t_hi, z1t_lo)
                if valid(i - 1):
                    project_out(i)
                if valid(i):
                    largest(i, 1)
                if valid(i + 1):
                    fill_lo(i, "k1")
                if valid(i):
                    select(i, 1)
                if valid(i + 1):
                    fill_lo(i, "k0")
                if valid(i):
                    weights_t_lo(i, 0)
                if valid(i - 1):
                    normal(i - 1, mv2, rs2, z2, rstd2, z2_ok)
                if valid(i + 1):
                    fill_lo(i, "q1")
                if valid(i):
                    normalise(i, 0)
                if valid(i - 1):
                    z_lo(i - 1, z2t, z2t_hi, z2t_lo)
                if valid(i + 2):
                    embed_out(i)
                if first(i, FIRST):
                    for n in FILLS:
                        weights_lo(n)
                if first(i, 0):
                    weights_lo("out")
                if first(i, 1):
                    weights_lo("rec")
                if valid(i - 2):
                    update(i - 2, 1)
                if valid(i):
                    normalise(i, 1)
                    weights_t_lo(i, 1)
                if valid(i + 1):
                    fill_lo(i, "q0")
                if valid(i):
                    normalise(i, 2)
                if valid(i + 1):
                    fill_lo(i, "v0")
                if valid(i + 2):
                    normal(i + 2, mv1, rs1, z1, rstd1, z1_ok)
                if valid(i):
                    att_lo(i, 0)
                    normalise(i, 3)
                if first(i, 0):
                    weights_lo("ffn")
                    start_state()
                if valid(i - 1):
                    update(i - 1, 0)
                if valid(i):
                    att_lo(i, 1)
                if valid(i + 1):
                    fill_lo(i, "v1")

            for t in (*qd, *pd, *vn, zero):
                v = t[:].rearrange("p a b c -> p (a b c)") if len(t.shape) == 4 else (
                    flat(t) if len(t.shape) == 3 else t[:])
                eng.memset(v.bitcast(F32), 0.0).then_inc(zeroed, 1)
            eng.wait_ge(zeroed, 7)
            eng.memset(vn[0][:, :, HD:HD + 1], SW / SA)
            weights_lo("tok0")
            weights_lo("tok1")
            eng.wait_ge(ld_small, 80)
            iterate(eng, body)
            eng.wait_ge(st_ok[1], PAIRS)
            for n in range(2):
                eng.tensor_copy(state_d[n][:], state_h[n][:].unsqueeze(2).broadcast_to([P, KD, 2, TOKENS])
                                ).then_inc(dup_ok, 1)
            eng.wait_ge(cu_done, 1)
            eng.scalar_tensor_tensor(out=cub[:], in0=p_a[:, 0:DIM], scalar=1 / SW, in1=ffnbo[:],
                                     op0=ALU.mult, op1=ALU.add).then_inc(cub_ok, 1)
            eng.wait_ge(cub_ok, 1)
            eng.wait_ge(xo_ok, PAIRS)

            def add_state(n):
                if n < FIN:
                    eng.tensor_tensor(xo_all[:, FP * n:FP * n + FP, :], xo_all[:, FP * n:FP * n + FP, :],
                                      cub[:].unsqueeze(1).broadcast_to([P, FP, DIM]), ALU.add).then_inc(fin_in, 1)

            add_state(0)
            add_state(1)
            for n in range(FIN):
                add_state(n + 2)
                if n not in FIN_POOL:
                    eng.wait_ge(fin_tanh, n + 1)
                    eng.tensor_tensor(h_all[:, FP * n:FP * n + FP, :], xo_all[:, FP * n:FP * n + FP, :],
                                      h_all[:, FP * n:FP * n + FP, :], ALU.add).then_inc(fin_ok[n], 1)


def kernel(**inputs):
    import numpy as np
    import concourse.bacc as bacc
    from concourse import mybir as mb
    from concourse.bass_utils import run_bass_kernel_spmd

    a = {k: np.asarray(v) for k, v in inputs.items()}

    def rows(w):
        o, k = w.shape
        return np.ascontiguousarray(w.T.reshape(k // P, P, o).transpose(1, 0, 2))

    x = a["x"].reshape(PAIRS, 2, 3, 8, 16, 8, 16).transpose(0, 2, 4, 6, 1, 3, 5)
    x = x.reshape(PAIRS, XC, P, P).transpose(0, 2, 1, 3).reshape(PAIRS, P, XC * P)
    arrays = {
        "in_x": np.ascontiguousarray(x),
        "in_tok_w": rows(a["L0_tok_W"]),
        "in_tok_b": a["L0_tok_b"],
        "in_qkv_w": rows(a["L0_attn_W_qkv"]),
        "in_out_w": rows(a["L0_attn_W_out"]),
        "in_out_b": a["L0_attn_b_out"],
        "in_ffn_w": rows(np.concatenate([a[f"L0_ffn_w{g}"] for g in "fico"])),
        "in_rec_w": rows(np.concatenate([a[f"L0_ffn_u{g}"] for g in "fico"])),
        "in_gate_b": np.concatenate([a[f"L0_ffn_b{g}"] for g in "fic"]).reshape(GM, P).T.copy(),
        "in_ffn_bo": a["L0_ffn_bo"],
        "in_c": np.ascontiguousarray(a["L0_ffn_in_c"].reshape(KD, P).T),
    }
    nc = bacc.Bacc("TRN2", target_bir_lowering=False, num_devices=1)
    args = [nc.dram_tensor(n, v.shape, mb.dt.from_np(v.dtype), kind="ExternalInput").ap() for n, v in arrays.items()]
    args.append(nc.dram_tensor("out_h", (PAIRS, P, DIM), mb.dt.float32, kind="ExternalOutput").ap())
    build_program(nc, *args)
    r = run_bass_kernel_spmd(nc, [arrays], core_ids=[0])
    return r.results[0]["out_h"].reshape(IMAGES, TOKENS, DIM)
```

```python
from contextlib import ExitStack

import concourse.bass as bass
from concourse import mybir

F32 = mybir.dt.float32
F16 = mybir.dt.float16
I32 = mybir.dt.int32
ALU = mybir.AluOpType
ACT = mybir.ActivationFunctionType

P = 128
IMAGES, TOKENS, DIM = 64, 64, 256
PAIRS = IMAGES // 2
PATCH = 3 * 16 * 16
XC = PATCH // P
HEADS, HD = 16, 64
INNER = HEADS * HD
HP = HEADS // 2
KD = DIM // P
GATES = 3 * DIM
GM = GATES // P
TOPK = max(1, int(0.1 * TOKENS))
EPS = 1e-5
NEWTON = 3
RSQRT_STEPS = 2 + 3 * NEWTON
RSQRT_BITS = float(0x5F3759DF)
VW = HD + 2

SW = 64.0
SQ = 4.0
SE = DIM ** -0.5 / (SQ * SQ)
SA = 4.0
SP = 256.0
SU = SW / 2

FIN = 16
FP = PAIRS // FIN
FIN_STATE = (12, 13, 14, 15)
FIN_LAST = (3, 5, 7, 9, 11, 13)

FIRST, LAST = -2, PAIRS + 1
LOOP_FROM, LOOP_TO = 3, PAIRS - 2

FILLS = ("k1", "q0", "q1", "k0", "v0", "v1")
WEIGHTS = ("tok0", "tok1", *FILLS, "out0", "out1", "ffn0", "ffn1", "rec0", "rec1")


def count(name):
    return WEIGHTS.index(name) + 1


def column(name):
    return INNER * "qkv".index(name[0]) + 512 * int(name[1])


def build_program(nc, x, tok_w, tok_b, qkv_w, out_w, out_b, ffn_w, rec_w, gate_b, ffn_bo, in_c, out):
    with ExitStack() as ctx:
        def sb(name, shape, dt):
            return ctx.enter_context(nc.sbuf_tensor(name, shape, dt))

        def bank(name):
            return ctx.enter_context(nc.psum_tensor(name, [P, 512], F32))

        def sem(name):
            return ctx.enter_context(nc.semaphore(name))

        tokw = [sb(f"tokw_{s}", [P, XC, DIM], F16) for s in ("hi", "lo")]
        qkvw = [sb(f"qkvw_{s}", [P, KD, 3 * INNER], F16) for s in ("hi", "lo")]
        outw = [sb(f"outw_{s}", [P, HP, DIM], F16) for s in ("hi", "lo")]
        ffnw = [sb(f"ffnw_{s}", [P, KD, 4 * DIM], F16) for s in ("hi", "lo")]
        recw = [sb(f"recw_{s}", [P, KD, 4 * DIM], F16) for s in ("hi", "lo")]
        gateb = sb("gateb", [P, GM], F32)
        tokb = sb("tokb", [P, DIM], F32)
        outb = sb("outb", [P, DIM], F32)
        ffnbo = sb("ffnbo", [P, DIM], F32)
        c0 = sb("c0", [P, KD], F32)
        ident = sb("ident", [P, P], F32)
        h_all = sb("h_all", [P, PAIRS, DIM], F32)
        xo_all = sb("xo_all", [P, PAIRS, DIM], F32)
        xo_flat = xo_all[:, :, :].rearrange("p a d -> p (a d)")
        h_flat = h_all[:, :, :].rearrange("p a d -> p (a d)")
        tok_st = xo_flat[:, 0:XC * DIM].rearrange("p (c d) -> p c d", d=DIM)
        qkv_st = xo_flat[:, XC * DIM:XC * DIM + KD * 3 * INNER].rearrange("p (c d) -> p c d", d=3 * INNER)
        tail = 8 * DIM
        out_st = h_flat[:, tail:tail + HP * DIM].rearrange("p (c d) -> p c d", d=DIM)
        ffn_st = h_flat[:, tail + HP * DIM:tail + HP * DIM + KD * 4 * DIM].rearrange("p (c d) -> p c d", d=4 * DIM)
        rec_st = h_flat[:, tail + HP * DIM + KD * 4 * DIM:tail + HP * DIM + 2 * KD * 4 * DIM].rearrange(
            "p (c d) -> p c d", d=4 * DIM)
        half = XC // 2
        split = {f"tok{n}": (tok_st[:, n * half:(n + 1) * half, :],
                             [t[:, n * half:(n + 1) * half, :] for t in tokw], SW) for n in range(2)}
        split.update({n: (qkv_st[:, :, column(n):column(n) + 512],
                          [t[:, :, column(n):column(n) + 512] for t in qkvw], SW) for n in FILLS})
        for name, st, pair, scale in (("out", out_st, outw, SW), ("ffn", ffn_st, ffnw, SW), ("rec", rec_st, recw, SU)):
            c = st.shape[1] // 2
            split.update({f"{name}{n}": (st[:, n * c:(n + 1) * c, :], [t[:, n * c:(n + 1) * c, :] for t in pair], scale)
                          for n in range(2)})
        xf = sb("xf", [P, XC * P], F32)
        xs = [sb(f"xs_{s}", [P, XC, P], F16) for s in ("hi", "lo")]
        h1 = sb("h1", [P, DIM], F32)
        h2 = sb("h2", [P, DIM], F32)
        z1 = sb("z1", [P, DIM], F32)
        z2 = sb("z2", [P, DIM], F32)
        st1 = sb("st1", [P, 6], F32)
        st2 = sb("st2", [P, 6], F32)
        mv1 = sb("mv1", [P, 2], F32)
        mv2 = sb("mv2", [P, 2], F32)
        rs1 = sb("rs1", [P, 1], F32)
        rs2 = sb("rs2", [P, 1], F32)
        nt = sb("nt", [P, 1], F32)
        z1t = [sb(f"z1t_{s}", [P, KD, P], F16) for s in ("hi", "lo")]
        z2t = [sb(f"z2t_{s}", [P, KD, P], F16) for s in ("hi", "lo")]
        qd = [sb(f"qd_{s}", [P, HP, 2, P], F16) for s in ("hi", "lo")]
        kt = [sb(f"kt_{s}", [P, HP, P], F16) for s in ("hi", "lo")]
        vn = [sb(f"vn_{s}", [P, HEADS, VW], F16) for s in ("hi", "lo")]
        top8 = [sb(f"top8_{n}", [P, 8, 8], F32) for n in range(2)]
        ebias = [sb(f"ebias_{n}", [P, 8], F32) for n in range(2)]
        keep = [sb(f"keep_{n}", [P, 512], F16) for n in range(2)]
        expo = [sb(f"expo_{n}", [P, 512], F32) for n in range(2)]
        wts = [sb(f"wts_{n}", [P, 512], F32) for n in range(2)]
        pd = [sb(f"pd_{s}", [P, 8, P], F16) for s in ("hi", "lo")]
        rden = sb("rden", [P, 4, 4], F32)
        att = sb("att", [P, HEADS, HD], F32)
        att_t = [sb(f"att_t_{s}", [P, HP, P], F16) for s in ("hi", "lo")]
        tfi = sb("tfi", [P, 2 * P], F32)
        tg = sb("tg", [P, P], F32)
        fs = sb("fs", [P, P], F32)
        ig = sb("ig", [P, P], F32)
        state = sb("state", [P, KD * TOKENS], F32)
        state_h = [sb(f"state_{s}", [P, KD, TOKENS], F16) for s in ("hi", "lo")]
        state_d = [sb(f"state_d_{s}", [P, KD, 2, TOKENS], F16) for s in ("hi", "lo")]
        cub = sb("cub", [P, DIM], F32)
        zero = sb("zero", [P, TOKENS], F32)

        p_fi, p_g = bank("p_fi"), bank("p_g")
        p_a, p_b = bank("p_a"), bank("p_b")
        p_s = [bank("p_s0"), bank("p_s1")]
        p_t = bank("p_t")
        p_av = bank("p_av")

        ld = {n: sem(f"ld_{n}") for n in WEIGHTS}
        ld_small = sem("ld_small")
        ld_x = sem("ld_x")
        passed = sem("passed")
        made = sem("made")
        zeroed = sem("zeroed")
        bias_ok = sem("bias_ok")
        ident_ok = sem("ident_ok")
        wh = sem("wh")
        wl = sem("wl")
        setup_ok = sem("setup_ok")
        x_hi, x_lo = sem("x_hi"), sem("x_lo")
        tok_done, h1_ok, ln1, z1_ok = sem("tok_done"), sem("h1_ok"), sem("ln1"), sem("z1_ok")
        rstd1, rstd2 = sem("rstd1"), sem("rstd2")
        res_ok, kept = sem("res_ok"), sem("kept")
        z1t_done, z1t_hi, z1t_lo = sem("z1t_done"), sem("z1t_hi"), sem("z1t_lo")
        f_done = {n: sem(f"{n}_done") for n in FILLS}
        f_hi = {n: sem(f"{n}_hi") for n in FILLS}
        f_lo = {n: sem(f"{n}_lo") for n in FILLS}
        s_done = [sem(f"s_done{n}") for n in range(2)]
        max_ok = [sem(f"max_ok{n}") for n in range(2)]
        ebias_ok = [sem(f"ebias_ok{n}") for n in range(2)]
        keep_ok = [sem(f"keep_ok{n}") for n in range(2)]
        exp_ok = [sem(f"exp_ok{n}") for n in range(2)]
        wts_ok = [sem(f"wts_ok{n}") for n in range(2)]
        pt_done = [sem(f"pt_done{n}") for n in range(2)]
        pt_hi = [sem(f"pt_hi{n}") for n in range(2)]
        pt_lo = [sem(f"pt_lo{n}") for n in range(2)]
        av_done = [sem(f"av_done{n}") for n in range(4)]
        rden_ok = [sem(f"rden_ok{n}") for n in range(4)]
        att_ok = [sem(f"att_ok{n}") for n in range(4)]
        at_done = [sem(f"at_done{n}") for n in range(2)]
        at_hi = [sem(f"at_hi{n}") for n in range(2)]
        at_lo = [sem(f"at_lo{n}") for n in range(2)]
        y_done, h2_ok, ln2, z2_ok = sem("y_done"), sem("h2_ok"), sem("ln2"), sem("z2_ok")
        z2t_done, z2t_hi, z2t_lo = sem("z2t_done"), sem("z2t_hi"), sem("z2t_lo")
        xo_done, xo_ok = sem("xo_done"), sem("xo_ok")
        rec_done = [sem(f"rec_done{n}") for n in range(2)]
        gate_ok = [sem(f"gate_ok{n}") for n in range(2)]
        rec_step = [sem(f"rec_step{n}") for n in range(2)]
        st_ok = [sem(f"st_ok{n}") for n in range(2)]
        st0 = sem("st0")
        dup_ok, cu_done, cub_ok = sem("dup_ok"), sem("cu_done"), sem("cub_ok")
        fin_tanh, stored = sem("fin_tanh"), sem("stored")
        fin_in = [sem(f"fin_in{n}") for n in range(FIN)]
        fin_ok = [sem(f"fin_ok{n}") for n in range(FIN)]

        def only(i, at):
            return isinstance(i, int) and i == at

        def gate(m):
            return p_fi[:, m * P:(m + 1) * P] if m < 4 else p_g[:, (m - 4) * P:(m - 3) * P]

        def valid(p):
            return not isinstance(p, int) or 0 <= p < PAIRS

        turns_a = [(h2_ok, -1), (f_lo["q0"], 1), (f_lo["q1"], 1), (f_lo["v1"], 1)]
        turns_b = [(f_lo["k1"], 1), (h1_ok, 2), (f_lo["k0"], 1), (f_lo["v0"], 1), (xo_ok, -1)]
        turns_t = [(z1t_lo, 1), (pt_lo[0], 0), (z2t_lo, -1), (pt_lo[1], 0), (at_lo[0], 0), (at_lo[1], 0)]
        turns_v = [(att_ok[0], 0), (att_ok[1], 0), (att_ok[2], 0), (att_ok[3], 0)]
        home = {n: (p_a, turns_a) for n in ("project", "q0", "q1", "v1")}
        home.update({n: (p_b, turns_b) for n in ("k1", "embed", "k0", "v0", "out_x")})

        def bank_free(eng, turns, reader, i):
            at = [t[0] is reader for t in turns].index(True)
            n = i
            while True:
                at -= 1
                if at < 0:
                    at, n = len(turns) - 1, n - 1
                if isinstance(n, int) and n < FIRST:
                    return
                s, lag = turns[at]
                if valid(n + lag):
                    eng.wait_ge(s, n + lag + 1)
                    return

        def wait_alone(eng, s, value):
            eng.wait_ge(s, value)
            eng.sem_inc(passed, 1)

        def iterate(eng, body):
            for i in range(FIRST, LOOP_FROM):
                body(i)
            with eng.Fori(LOOP_FROM, LOOP_TO) as i:
                body(i)
            for i in range(LOOP_TO, LAST + 1):
                body(i)

        block = ctx.enter_context(nc.Block())

        @block.sync
        def _(eng):
            eng.dma_start(xf[:], x[0]).then_inc(ld_x, 16)
            for n in range(2):
                eng.dma_start(split[f"tok{n}"][0], tok_w[:, n * half:(n + 1) * half, :]).then_inc(ld[f"tok{n}"], 16)
            eng.dma_start(tokb[:], tok_b.partition_broadcast(P)).then_inc(ld_small, 16)
            eng.dma_start(outb[:], out_b.partition_broadcast(P)).then_inc(ld_small, 16)
            eng.dma_start(ffnbo[:], ffn_bo.partition_broadcast(P)).then_inc(ld_small, 16)
            eng.dma_start(c0[:], in_c).then_inc(ld_small, 16)
            eng.dma_start(gateb[:], gate_b).then_inc(ld_small, 16)
            for n in FILLS:
                eng.dma_start(split[n][0], qkv_w[:, :, column(n):column(n) + 512]).then_inc(ld[n], 16)

            def patches(p):
                eng.wait_ge(x_hi, p)
                eng.wait_ge(x_lo, p)
                eng.dma_start(xf[:], x[p]).then_inc(ld_x, 16)

            patches(1)
            for name, w in (("out", out_w), ("ffn", ffn_w), ("rec", rec_w)):
                for n in range(2):
                    st = split[f"{name}{n}"][0]
                    c = st.shape[1]
                    eng.dma_start(st, w[:, n * c:(n + 1) * c, :]).then_inc(ld[f"{name}{n}"], 16)
            with eng.Fori(2, PAIRS) as p:
                patches(p)
            for n in range(FIN):
                eng.wait_ge(fin_ok[n], 1)
                eng.dma_start(out[FP * n:FP * n + FP].rearrange("a p d -> p a d"),
                              h_all[:, FP * n:FP * n + FP, :]).then_inc(stored, 16)
            eng.wait_ge(stored, 16 * FIN)

        @block.gpsimd
        def _(eng):
            eng.memset(ident[:], 0.0).then_inc(made, 1)
            eng.wait_ge(made, 1)
            eng.affine_select(out=ident[:], in_=ident[:], compare_op=ALU.not_equal, fill=1.0, base=0,
                              pattern=[[-1, P]], channel_multiplier=1).then_inc(ident_ok, 1)

            def halve_biases():
                eng.wait_ge(ld_small, 80)
                eng.tensor_scalar(gateb[:, 0:4], gateb[:, 0:4], 0.5, None, ALU.mult).then_inc(bias_ok, 1)

            def patches_lo(i):
                eng.wait_ge(x_hi, i + 3)
                eng.tensor_tensor(xs[1][:].rearrange("p c t -> p (c t)"), xf[:],
                                  xs[0][:].rearrange("p c t -> p (c t)"), ALU.subtract).then_inc(x_lo, 1)

            def add_bias(i):
                wait_alone(eng, h1_ok, i + 3)
                eng.tensor_tensor(h_all[:, i + 2, :], h1[:], outb[:], ALU.add).then_inc(res_ok, 1)

            def exp_bias(i, hf):
                wait_alone(eng, max_ok[hf], i + 1)
                eng.tensor_scalar(ebias[hf][:], top8[hf][:, :, 0], -SE, None, ALU.mult).then_inc(ebias_ok[hf], 1)

            def inverse_deviation(p, mv, rs, chain, ok):
                var, y, t = mv[:, 1:2], rs[:], nt[:]
                at = RSQRT_STEPS * p
                wait_alone(eng, chain, 2 * p + 2)
                eng.tensor_scalar(var, var, EPS, None, ALU.add).then_inc(ok, 1)
                wait_alone(eng, ok, at + 1)
                eng.tensor_scalar(y.bitcast(I32), var.bitcast(I32), -0.5, RSQRT_BITS, ALU.mult, ALU.add).then_inc(ok, 1)
                for n in range(NEWTON):
                    wait_alone(eng, ok, at + 3 * n + 2)
                    eng.tensor_scalar(t, y, y, var, ALU.mult, ALU.mult).then_inc(ok, 1)
                    wait_alone(eng, ok, at + 3 * n + 3)
                    eng.tensor_scalar(t, t, -0.5, 1.5, ALU.mult, ALU.add).then_inc(ok, 1)
                    wait_alone(eng, ok, at + 3 * n + 4)
                    eng.tensor_tensor(y, y, t, ALU.mult).then_inc(ok, 1)

            def normal(p, h, mv, rs, z, rstd, turned, z_ok):
                if not isinstance(p, int) or p > 0:
                    wait_alone(eng, turned, p)
                wait_alone(eng, rstd, RSQRT_STEPS * (p + 1))
                eng.tensor_scalar(z[:], h[:], mv[:, 0:1], rs[:], ALU.subtract, ALU.mult).then_inc(z_ok, 1)

            def mask(i, hf):
                eng.wait_ge(exp_ok[hf], i + 1)
                eng.wait_ge(keep_ok[hf], i + 1)
                eng.tensor_tensor(wts[hf][:], expo[hf][:], keep[hf][:], ALU.mult).then_inc(wts_ok[hf], 1)

            def body(i):
                if valid(i):
                    exp_bias(i, 0)
                if valid(i + 2):
                    patches_lo(i)
                if only(i, FIRST):
                    halve_biases()
                if valid(i):
                    exp_bias(i, 1)
                    mask(i, 0)
                if valid(i - 1):
                    inverse_deviation(i - 1, mv2, rs2, ln2, rstd2)
                    normal(i - 1, h2, mv2, rs2, z2, rstd2, z2t_done, z2_ok)
                if valid(i):
                    mask(i, 1)
                if valid(i + 2):
                    inverse_deviation(i + 2, mv1, rs1, ln1, rstd1)
                    normal(i + 2, h1, mv1, rs1, z1, rstd1, z1t_done, z1_ok)
                    add_bias(i)
            iterate(eng, body)
            eng.wait_ge(kept, PAIRS)
            eng.wait_ge(cub_ok, 1)
            eng.wait_ge(xo_ok, PAIRS)
            for n in FIN_STATE:
                eng.tensor_tensor(xo_all[:, FP * n:FP * n + FP, :], xo_all[:, FP * n:FP * n + FP, :],
                                  cub[:].unsqueeze(1).broadcast_to([P, FP, DIM]), ALU.add).then_inc(fin_in[n], 1)
            for n in FIN_LAST:
                eng.wait_ge(fin_tanh, n + 1)
                eng.tensor_tensor(h_all[:, FP * n:FP * n + FP, :], xo_all[:, FP * n:FP * n + FP, :],
                                  h_all[:, FP * n:FP * n + FP, :], ALU.add).then_inc(fin_ok[n], 1)

        @block.tensor
        def _(eng):
            def mm3(o, stat, mov, start, stop, skip=False):
                sh, sl = stat
                mh, ml = mov
                eng.matmul(o, sh, mh, start=start, stop=False, skip_group_check=skip)
                eng.matmul(o, sh, ml, start=False, stop=False, skip_group_check=skip)
                return eng.matmul(o, sl, mh, start=False, stop=stop, skip_group_check=skip)

            def part(pair, f):
                return [f(t) for t in pair]

            def embed(i):
                p = i + 2
                eng.wait_ge(x_hi, p + 1)
                eng.wait_ge(x_lo, p + 1)
                bank_free(eng, home["embed"][1], h1_ok, i)
                for c in range(XC):
                    if only(i, FIRST) and c % half == 0:
                        eng.wait_ge(wl, count(f"tok{c // half}"))
                    last = mm3(home["embed"][0][:, 0:DIM], part(xs, lambda t: t[:, c, :]),
                               part(tokw, lambda t: t[:, c, :]), c == 0, c == XC - 1)
                last.then_inc(tok_done, 1)

            def turn_z(i, z, ready, turns, reader, done, p):
                eng.wait_ge(ready, p + 1)
                bank_free(eng, turns, reader, i)
                for k in range(KD):
                    last = eng.transpose(p_t[:, k * P:(k + 1) * P], z[:, k * P:(k + 1) * P], ident[:])
                last.then_inc(done, 1)

            def fill(i, name):
                p = i + 1
                bnk, turns = home[name]
                if name == FILLS[0]:
                    eng.wait_ge(z1t_lo, p + 1)
                bank_free(eng, turns, f_lo[name], i)
                if only(p, 0):
                    eng.wait_ge(wl, count(name))
                o = column(name)
                if name[0] == "v":
                    for k in range(KD):
                        last = mm3(bnk[:, :], part(z1t, lambda t: t[:, k, :]),
                                   part(qkvw, lambda t: t[:, k, o:o + 512]), k == 0, k == KD - 1)
                else:
                    for c in range(4):
                        for k in range(KD):
                            last = mm3(bnk[:, c * P:(c + 1) * P],
                                       part(qkvw, lambda t: t[:, k, o + c * P:o + (c + 1) * P]),
                                       part(z1t, lambda t: t[:, k, :]), k == 0, k == KD - 1)
                last.then_inc(f_done[name], 1)

            def scores(i, hf):
                eng.wait_ge(f_lo[f"q{hf}"], i + 1)
                eng.wait_ge(f_lo[f"k{hf}"], i + 1)
                if not isinstance(i, int) or i > 0:
                    eng.wait_ge(exp_ok[hf], i)
                for c in range(4):
                    for m in range(2):
                        last = mm3(p_s[hf][:, (2 * c + m) * 64:(2 * c + m + 1) * 64],
                                   part(qd, lambda t: t[:, 4 * hf + c, m, :]),
                                   part(kt, lambda t: t[:, 4 * hf + c, 64 * m:64 * m + 64]), True, True)
                last.then_inc(s_done[hf], 1)

            def turn_weights(i, hf):
                eng.wait_ge(wts_ok[hf], i + 1)
                bank_free(eng, turns_t, pt_lo[hf], i)
                for c in range(4):
                    last = eng.transpose(p_t[:, c * P:(c + 1) * P], wts[hf][:, c * P:(c + 1) * P], ident[:])
                last.then_inc(pt_done[hf], 1)

            def attend(i, qr):
                hf = qr // 2
                eng.wait_ge(pt_lo[hf], i + 1)
                eng.wait_ge(f_lo[f"v{hf}"], i + 1)
                bank_free(eng, turns_v, att_ok[qr], i)
                for n in range(4):
                    head = 4 * qr + n
                    last = mm3(p_av[:, n * VW:(n + 1) * VW], part(pd, lambda t: t[:, head % 8, :]),
                               part(vn, lambda t: t[:, head, :]), True, True)
                last.then_inc(av_done[qr], 1)

            def turn_att(i, hf):
                eng.wait_ge(att_ok[2 * hf + 1], i + 1)
                bank_free(eng, turns_t, at_lo[hf], i)
                for c in range(4):
                    j = 4 * hf + c
                    last = eng.transpose(p_t[:, c * P:(c + 1) * P],
                                         att[:, 2 * j:2 * j + 2, :].rearrange("p h d -> p (h d)"), ident[:])
                last.then_inc(at_done[hf], 1)

            def project(i):
                p = i - 1
                eng.wait_ge(at_lo[0], p + 1)
                eng.wait_ge(at_lo[1], p + 1)
                bank_free(eng, home["project"][1], h2_ok, i)
                if only(p, 0):
                    eng.wait_ge(wl, count("out1"))
                for j in range(HP):
                    last = mm3(home["project"][0][:, 0:DIM], part(att_t, lambda t: t[:, j, :]),
                               part(outw, lambda t: t[:, j, :]), j == 0, j == HP - 1)
                last.then_inc(y_done, 1)

            def gates_x(i):
                p = i - 1
                eng.wait_ge(z2t_lo, p + 1)
                if not isinstance(p, int) or p > 0:
                    for s in range(2):
                        eng.wait_ge(gate_ok[s], GM * p)
                if only(p, 0):
                    eng.wait_ge(wl, count("ffn1"))
                for m in range(GM):
                    for k in range(KD):
                        for wgt, zz in ((0, 0), (0, 1), (1, 0)):
                            eng.matmul(gate(m), ffnw[wgt][:, k, m * P:(m + 1) * P], z2t[zz][:, k, :],
                                       start=(m in (0, 4) and k == 0 and wgt == zz == 0), stop=False,
                                       skip_group_check=True)

            def out_x(i):
                bank_free(eng, home["out_x"][1], xo_ok, i)
                for k in range(KD):
                    last = mm3(home["out_x"][0][:, 0:DIM], part(z2t, lambda t: t[:, k, :]),
                               part(ffnw, lambda t: t[:, k, GATES:GATES + DIM]), k == 0, k == KD - 1)
                last.then_inc(xo_done, 1)

            def recur(p, s):
                if s == 1:
                    eng.wait_ge(st_ok[0], p + 1)
                elif isinstance(p, int) and p == 0:
                    eng.wait_ge(setup_ok, 1)
                    eng.wait_ge(wl, count("rec1"))
                else:
                    eng.wait_ge(st_ok[1], p)
                for m in range(GM):
                    for k in range(KD):
                        last = mm3(gate(m)[:, 64 * s:64 * s + 64],
                                   part(recw, lambda t: t[:, k, m * P:(m + 1) * P]),
                                   part(state_h, lambda t: t[:, k, :]), False, m == GM - 1 and k == KD - 1, True)
                last.then_inc(rec_done[s], 1)

            def body(i):
                if valid(i):
                    scores(i, 0)
                    scores(i, 1)
                if valid(i + 1):
                    turn_z(i, z1, z1_ok, turns_t, z1t_lo, z1t_done, i + 1)
                if valid(i - 1):
                    project(i)
                if valid(i + 1):
                    fill(i, "k1")
                    fill(i, "q0")
                if valid(i):
                    turn_weights(i, 0)
                if valid(i + 2):
                    embed(i)
                if only(i, PAIRS):
                    gates_x(i - 1)
                    recur(i - 2, 0)
                if valid(i - 2):
                    recur(i - 2, 1)
                if valid(i + 1):
                    fill(i, "q1")
                if valid(i):
                    attend(i, 0)
                if valid(i - 1):
                    turn_z(i, z2, z2_ok, turns_t, z2t_lo, z2t_done, i - 1)
                if valid(i + 1):
                    fill(i, "k0")
                if valid(i):
                    attend(i, 1)
                    turn_weights(i, 1)
                if valid(i - 1) and not only(i, PAIRS - 1):
                    gates_x(i)
                    recur(i - 1, 0)
                if valid(i):
                    turn_att(i, 0)
                    attend(i, 2)
                if valid(i + 1):
                    fill(i, "v0")
                if valid(i):
                    attend(i, 3)
                if valid(i + 1):
                    fill(i, "v1")
                if valid(i):
                    turn_att(i, 1)
                if valid(i - 1):
                    out_x(i)

            eng.wait_ge(ident_ok, 1)
            iterate(eng, body)
            eng.wait_ge(dup_ok, 2)
            for k in range(KD):
                last = mm3(p_a[:, 0:DIM], part(state_d, lambda t: t[:, k, :, :].rearrange("p a t -> p (a t)")),
                           part(recw, lambda t: t[:, k, GATES:GATES + DIM]), k == 0, k == KD - 1)
            last.then_inc(cu_done, 1)

        @block.scalar
        def _(eng):
            def weights_hi(name):
                st, pair, scale = split[name]
                eng.wait_ge(ld[name], 16)
                eng.activation(pair[0], st, ACT.Copy, scale=scale).then_inc(wh, 1)

            def flat(t):
                return t[:].rearrange("p a b -> p (a b)")

            def patches_hi(i):
                p = i + 2
                eng.wait_ge(ld_x, 16 * (p + 1))
                if not isinstance(p, int) or p > 0:
                    eng.wait_ge(tok_done, p)
                eng.activation(flat(xs[0]), xf[:], ACT.Copy).then_inc(x_hi, 1)

            def fill_hi(i, name):
                p = i + 1
                hf = int(name[1])
                src = home[name][0]
                eng.wait_ge(f_done[name], p + 1)
                if name[0] == "q":
                    for u in range(2):
                        r = slice(64 * u, 64 * u + 64)
                        last = eng.activation(
                            qd[0][r, 4 * hf:4 * hf + 4, :, r].rearrange("p c m t -> p (c m) t"),
                            src[r, :].rearrange("p (c t) -> p c t", t=64), ACT.Copy, scale=SQ / SW)
                    last.then_inc(f_hi[name], 1)
                elif name[0] == "k":
                    eng.activation(kt[0][:, 4 * hf:4 * hf + 4, :].rearrange("p c t -> p (c t)"), src[:, :],
                                   ACT.Copy, scale=SQ / SW).then_inc(f_hi[name], 1)
                else:
                    eng.activation(vn[0][:, 8 * hf:8 * hf + 8, 0:HD], src[:, :].rearrange("p (h d) -> p h d", d=HD),
                                   ACT.Relu).then_inc(f_hi[name], 1)

            def exponentials(i, hf):
                eng.wait_ge(keep_ok[hf], i + 1)
                eng.wait_ge(ebias_ok[hf], i + 1)
                for u in range(8):
                    last = eng.activation(expo[hf][:, 64 * u:64 * u + 64], p_s[hf][:, 64 * u:64 * u + 64], ACT.Exp,
                                          bias=ebias[hf][:, u:u + 1], scale=SE)
                last.then_inc(exp_ok[hf], 1)

            def weights_t_hi(i, hf):
                eng.wait_ge(pt_done[hf], i + 1)
                for u in range(2):
                    r = slice(64 * u, 64 * u + 64)
                    last = eng.activation(pd[0][r, :, r], p_t[r, :].rearrange("p (h t) -> p h t", t=64),
                                          ACT.Copy, scale=SP)
                last.then_inc(pt_hi[hf], 1)

            def att_hi(p, hf):
                eng.wait_ge(at_done[hf], p + 1)
                eng.activation(att_t[0][:, 4 * hf:4 * hf + 4, :].rearrange("p c t -> p (c t)"), p_t[:, :],
                               ACT.Copy).then_inc(at_hi[hf], 1)

            def z_hi(p, zt, done, ok):
                eng.wait_ge(done, p + 1)
                eng.activation(flat(zt[0]), p_t[:, 0:DIM], ACT.Copy).then_inc(ok, 1)

            def gate_tanh(p, s):
                eng.wait_ge(rec_done[s], p + 1)
                if s == 1:
                    eng.wait_ge(st_ok[0], p + 1)
                elif not isinstance(p, int) or p > 0:
                    eng.wait_ge(st_ok[1], p)
                if only(p, 0) and s == 0:
                    eng.wait_ge(bias_ok, 1)
                for m in range(GM):
                    o, scale = (tfi[:, 64 * m:64 * m + 64], 0.5) if m < 4 else (tg[:, 64 * m - 256:64 * m - 192], 1.0)
                    eng.activation(o, gate(m)[:, 64 * s:64 * s + 64], ACT.Tanh, bias=gateb[:, m:m + 1],
                                   scale=scale / SW).then_inc(gate_ok[s], 1)

            def out_x_copy(i):
                eng.wait_ge(xo_done, i)
                eng.activation(xo_all[:, i - 1, :], home["out_x"][0][:, 0:DIM], ACT.Copy,
                               scale=1 / SW).then_inc(xo_ok, 1)

            def keep_residual(i):
                eng.wait_ge(h2_ok, i)
                eng.activation(h_all[:, i - 1, :], h2[:], ACT.Copy).then_inc(kept, 1)

            def body(i):
                if valid(i + 1):
                    z_hi(i + 1, z1t, z1t_done, z1t_hi)
                if valid(i + 2) and not only(i, FIRST):
                    patches_hi(i)
                if valid(i):
                    exponentials(i, 0)
                if valid(i + 1):
                    fill_hi(i, "k1")
                if only(i, -1):
                    weights_hi("out0")
                if valid(i + 1):
                    fill_hi(i, "q0")
                if only(i, -1):
                    weights_hi("out1")
                if valid(i):
                    weights_t_hi(i, 0)
                    exponentials(i, 1)
                if only(i, 0):
                    weights_hi("rec0")
                if only(i, PAIRS):
                    gate_tanh(i - 2, 0)
                if valid(i - 2):
                    gate_tanh(i - 2, 1)
                if valid(i - 1):
                    z_hi(i - 1, z2t, z2t_done, z2t_hi)
                if valid(i + 1):
                    fill_hi(i, "k0")
                if only(i, -1):
                    weights_hi("ffn0")
                if valid(i):
                    weights_t_hi(i, 1)
                if valid(i + 1):
                    fill_hi(i, "q1")
                if only(i, -1):
                    weights_hi("ffn1")
                if only(i, 0):
                    weights_hi("rec1")
                if valid(i - 1) and not only(i, PAIRS - 1):
                    gate_tanh(i - 1, 0)
                if valid(i):
                    att_hi(i, 0)
                if valid(i + 1):
                    fill_hi(i, "v0")
                if valid(i - 1):
                    keep_residual(i)
                if valid(i + 1):
                    fill_hi(i, "v1")
                if valid(i):
                    att_hi(i, 1)
                if valid(i - 1):
                    out_x_copy(i)

            patches_hi(FIRST)
            for n in ("tok0", "tok1", *FILLS):
                weights_hi(n)
            eng.wait_ge(zeroed, 7)
            iterate(eng, body)
            for n in range(FIN):
                eng.wait_ge(fin_in[n], 1)
                eng.activation(xo_all[:, FP * n:FP * n + FP, :], xo_all[:, FP * n:FP * n + FP, :],
                               ACT.Tanh).then_inc(fin_tanh, 1)

        @block.vector
        def _(eng):
            def flat(t):
                return t[:].rearrange("p a b -> p (a b)")

            def lo(o, src, scale, hi, op=ALU.mult):
                return eng.scalar_tensor_tensor(out=o, in0=src, scalar=scale, in1=hi, op0=op, op1=ALU.subtract)

            def weights_lo(name):
                st, pair, scale = split[name]
                eng.wait_ge(wh, count(name))
                lo(pair[1], st, scale, pair[0]).then_inc(wl, 1)

            def start_state():
                for k in range(KD):
                    last = eng.tensor_scalar(state[:, k * TOKENS:(k + 1) * TOKENS], zero[:, 0:TOKENS],
                                             c0[:, k:k + 1], 2.0, ALU.add, ALU.mult)
                last.then_inc(st0, 1)
                eng.wait_ge(st0, 1)
                eng.tensor_copy(flat(state_h[0]), state[:]).then_inc(st0, 1)
                eng.wait_ge(st0, 2)
                eng.tensor_tensor(flat(state_h[1]), state[:], flat(state_h[0]), ALU.subtract).then_inc(setup_ok, 1)

            def spread(p, h_ok, h, st, chain):
                wait_alone(eng, h_ok, p + 1)
                eng.bn_stats(st[:], h[:]).then_inc(chain, 1)

            def moments(p, st, mv, chain):
                wait_alone(eng, chain, 2 * p + 1)
                eng.bn_aggr(mv[:], st[:]).then_inc(chain, 1)

            def embed_out(i):
                p = i + 2
                eng.wait_ge(tok_done, p + 1)
                if not isinstance(p, int) or p > 0:
                    eng.wait_ge(z1_ok, p)
                    eng.wait_ge(res_ok, p)
                eng.scalar_tensor_tensor(out=h1[:], in0=home["embed"][0][:, 0:DIM], scalar=1 / SW, in1=tokb[:],
                                         op0=ALU.mult, op1=ALU.add).then_inc(h1_ok, 1)

            def project_out(i):
                p = i - 1
                eng.wait_ge(y_done, p + 1)
                eng.wait_ge(res_ok, p + 1)
                if not isinstance(p, int) or p > 0:
                    eng.wait_ge(z2_ok, p)
                    eng.wait_ge(kept, p)
                eng.scalar_tensor_tensor(out=h2[:], in0=home["project"][0][:, 0:DIM], scalar=1 / (SW * SA),
                                         in1=h_all[:, p, :], op0=ALU.mult, op1=ALU.add).then_inc(h2_ok, 1)

            def z_lo(p, zt, hi_ok, ok):
                eng.wait_ge(hi_ok, p + 1)
                eng.tensor_tensor(flat(zt[1]), p_t[:, 0:DIM], flat(zt[0]), ALU.subtract).then_inc(ok, 1)

            def fill_lo(i, name):
                p = i + 1
                hf = int(name[1])
                src = home[name][0]
                eng.wait_ge(f_hi[name], p + 1)
                if name[0] == "q":
                    for u in range(2):
                        r = slice(64 * u, 64 * u + 64)
                        o, hi = (t[r, 4 * hf:4 * hf + 4, :, r].rearrange("p c m t -> p (c m) t")
                                 for t in (qd[1], qd[0]))
                        last = lo(o, src[r, :].rearrange("p (c t) -> p c t", t=64), SQ / SW, hi)
                    last.then_inc(f_lo[name], 1)
                elif name[0] == "k":
                    o, hi = (t[:, 4 * hf:4 * hf + 4, :].rearrange("p c t -> p (c t)") for t in (kt[1], kt[0]))
                    lo(o, src[:, :], SQ / SW, hi).then_inc(f_lo[name], 1)
                else:
                    o, hi = (t[:, 8 * hf:8 * hf + 8, 0:HD] for t in (vn[1], vn[0]))
                    lo(o, src[:, :].rearrange("p (h d) -> p h d", d=HD), 0.0, hi, ALU.max).then_inc(f_lo[name], 1)

            def largest(i, hf):
                wait_alone(eng, s_done[hf], i + 1)
                for u in range(8):
                    last = eng.max(top8[hf][:, u, :], p_s[hf][:, 64 * u:64 * u + 64])
                last.then_inc(max_ok[hf], 1)

            def select(i, hf):
                eng.wait_ge(max_ok[hf], i + 1)
                eng.tensor_tensor(keep[hf][:].rearrange("p (u k) -> p u k", u=8),
                                  p_s[hf][:, :].rearrange("p (u k) -> p u k", u=8),
                                  top8[hf][:, :, TOPK - 1:TOPK].broadcast_to([P, 8, 64]),
                                  ALU.is_ge).then_inc(keep_ok[hf], 1)

            def weights_t_lo(i, hf):
                eng.wait_ge(pt_hi[hf], i + 1)
                for u in range(2):
                    r = slice(64 * u, 64 * u + 64)
                    last = lo(pd[1][r, :, r], p_t[r, :].rearrange("p (h t) -> p h t", t=64), SP, pd[0][r, :, r])
                last.then_inc(pt_lo[hf], 1)

            def invert(i, qr):
                eng.wait_ge(av_done[qr], i + 1)
                av = p_av[:, 0:4 * VW].rearrange("p (h w) -> p h w", w=VW)
                eng.reciprocal(rden[:, qr, :], av[:, :, HD]).then_inc(rden_ok[qr], 1)

            def normalise(i, qr):
                av = p_av[:, 0:4 * VW].rearrange("p (h w) -> p h w", w=VW)
                eng.wait_ge(rden_ok[qr], i + 1)
                eng.tensor_tensor(att[:, 4 * qr:4 * qr + 4, :], av[:, :, 0:HD],
                                  rden[:, qr, :].unsqueeze(2).broadcast_to([P, 4, HD]), ALU.mult
                                  ).then_inc(att_ok[qr], 1)

            def att_lo(p, hf):
                eng.wait_ge(at_hi[hf], p + 1)
                o, hi = (t[:, 4 * hf:4 * hf + 4, :].rearrange("p c t -> p (c t)") for t in (att_t[1], att_t[0]))
                eng.tensor_tensor(o, p_t[:, :], hi, ALU.subtract).then_inc(at_lo[hf], 1)

            def weigh(p, s):
                eng.wait_ge(gate_ok[s], GM * p + 2)
                eng.scalar_tensor_tensor(out=fs[:], in0=tfi[:, 0:P], scalar=1.0, in1=state[:],
                                         op0=ALU.add, op1=ALU.mult).then_inc(rec_step[s], 1)
                eng.wait_ge(gate_ok[s], GM * p + GM)
                eng.scalar_tensor_tensor(out=ig[:], in0=tfi[:, P:2 * P], scalar=1.0, in1=tg[:],
                                         op0=ALU.add, op1=ALU.mult).then_inc(rec_step[s], 1)

            def update(p, s):
                eng.wait_ge(rec_step[s], 4 * p + 2)
                for o in (state[:], flat(state_h[0])):
                    eng.scalar_tensor_tensor(out=o, in0=fs[:], scalar=0.5, in1=ig[:],
                                             op0=ALU.mult, op1=ALU.add).then_inc(rec_step[s], 1)

            def update_lo(p, s):
                eng.wait_ge(rec_step[s], 4 * p + 4)
                eng.tensor_tensor(flat(state_h[1]), state[:], flat(state_h[0]), ALU.subtract).then_inc(st_ok[s], 1)

            def body(i):
                if valid(i):
                    largest(i, 0)
                    select(i, 0)
                if valid(i + 1):
                    z_lo(i + 1, z1t, z1t_hi, z1t_lo)
                if valid(i):
                    largest(i, 1)
                if valid(i - 1):
                    project_out(i)
                    spread(i - 1, h2_ok, h2, st2, ln2)
                    moments(i - 1, st2, mv2, ln2)
                if valid(i + 1):
                    fill_lo(i, "k1")
                if only(i, -1):
                    weights_lo("out0")
                if valid(i):
                    select(i, 1)
                if valid(i + 1):
                    fill_lo(i, "q0")
                if only(i, -1):
                    weights_lo("out1")
                if valid(i):
                    weights_t_lo(i, 0)
                if valid(i + 2):
                    embed_out(i)
                    spread(i + 2, h1_ok, h1, st1, ln1)
                if valid(i):
                    invert(i, 0)
                    normalise(i, 0)
                if only(i, 0):
                    weights_lo("rec0")
                if only(i, PAIRS):
                    weigh(i - 2, 0)
                    update(i - 2, 0)
                    update_lo(i - 2, 0)
                if valid(i - 2):
                    weigh(i - 2, 1)
                if valid(i - 1):
                    z_lo(i - 1, z2t, z2t_hi, z2t_lo)
                if valid(i + 2):
                    moments(i + 2, st1, mv1, ln1)
                if only(i, FIRST):
                    for n in FILLS:
                        weights_lo(n)
                if valid(i - 2):
                    update(i - 2, 1)
                if valid(i):
                    invert(i, 1)
                if valid(i - 2):
                    update_lo(i - 2, 1)
                if valid(i + 1):
                    fill_lo(i, "k0")
                if only(i, -1):
                    weights_lo("ffn0")
                if valid(i):
                    normalise(i, 1)
                    weights_t_lo(i, 1)
                if valid(i + 1):
                    fill_lo(i, "q1")
                if only(i, -1):
                    weights_lo("ffn1")
                if valid(i):
                    invert(i, 2)
                    normalise(i, 2)
                if only(i, 0):
                    weights_lo("rec1")
                    start_state()
                if valid(i - 1) and not only(i, PAIRS - 1):
                    weigh(i - 1, 0)
                if valid(i):
                    att_lo(i, 0)
                    invert(i, 3)
                    normalise(i, 3)
                if valid(i + 1):
                    fill_lo(i, "v0")
                if valid(i - 1) and not only(i, PAIRS - 1):
                    update(i - 1, 0)
                if valid(i + 1):
                    fill_lo(i, "v1")
                if valid(i):
                    att_lo(i, 1)
                if valid(i - 1) and not only(i, PAIRS - 1):
                    update_lo(i - 1, 0)

            for t in (*qd, *pd, *vn, zero):
                v = t[:].rearrange("p a b c -> p (a b c)") if len(t.shape) == 4 else (
                    flat(t) if len(t.shape) == 3 else t[:])
                eng.memset(v.bitcast(F32), 0.0).then_inc(zeroed, 1)
            eng.wait_ge(zeroed, 7)
            eng.memset(vn[0][:, :, HD:HD + 1], SW / SA)
            weights_lo("tok0")
            weights_lo("tok1")
            eng.wait_ge(ld_small, 80)
            iterate(eng, body)
            eng.wait_ge(st_ok[1], PAIRS)
            for n in range(2):
                eng.tensor_copy(state_d[n][:], state_h[n][:].unsqueeze(2).broadcast_to([P, KD, 2, TOKENS])
                                ).then_inc(dup_ok, 1)
            eng.wait_ge(cu_done, 1)
            eng.scalar_tensor_tensor(out=cub[:], in0=p_a[:, 0:DIM], scalar=1 / SW, in1=ffnbo[:],
                                     op0=ALU.mult, op1=ALU.add).then_inc(cub_ok, 1)
            eng.wait_ge(cub_ok, 1)
            eng.wait_ge(xo_ok, PAIRS)

            def add_state(n):
                if n < FIN and n not in FIN_STATE:
                    eng.tensor_tensor(xo_all[:, FP * n:FP * n + FP, :], xo_all[:, FP * n:FP * n + FP, :],
                                      cub[:].unsqueeze(1).broadcast_to([P, FP, DIM]), ALU.add).then_inc(fin_in[n], 1)

            eng.wait_ge(kept, PAIRS)
            add_state(0)
            add_state(1)
            add_state(2)
            for n in range(FIN):
                add_state(n + 3)
                if n not in FIN_LAST:
                    eng.wait_ge(fin_tanh, n + 1)
                    eng.tensor_tensor(h_all[:, FP * n:FP * n + FP, :], xo_all[:, FP * n:FP * n + FP, :],
                                      h_all[:, FP * n:FP * n + FP, :], ALU.add).then_inc(fin_ok[n], 1)


def kernel(**inputs):
    import numpy as np
    import concourse.bacc as bacc
    from concourse import mybir as mb
    from concourse.bass_utils import run_bass_kernel_spmd

    a = {k: np.asarray(v) for k, v in inputs.items()}

    def rows(w):
        o, k = w.shape
        return np.ascontiguousarray(w.T.reshape(k // P, P, o).transpose(1, 0, 2))

    x = a["x"].reshape(PAIRS, 2, 3, 8, 16, 8, 16).transpose(0, 2, 4, 6, 1, 3, 5)
    x = x.reshape(PAIRS, XC, P, P).transpose(0, 2, 1, 3).reshape(PAIRS, P, XC * P)
    arrays = {
        "in_x": np.ascontiguousarray(x),
        "in_tok_w": rows(a["L0_tok_W"]),
        "in_tok_b": a["L0_tok_b"],
        "in_qkv_w": rows(a["L0_attn_W_qkv"]),
        "in_out_w": rows(a["L0_attn_W_out"]),
        "in_out_b": a["L0_attn_b_out"],
        "in_ffn_w": rows(np.concatenate([a[f"L0_ffn_w{g}"] for g in "fico"])),
        "in_rec_w": rows(np.concatenate([a[f"L0_ffn_u{g}"] for g in "fico"])),
        "in_gate_b": np.concatenate([a[f"L0_ffn_b{g}"] for g in "fic"]).reshape(GM, P).T.copy(),
        "in_ffn_bo": a["L0_ffn_bo"],
        "in_c": np.ascontiguousarray(a["L0_ffn_in_c"].reshape(KD, P).T),
    }
    nc = bacc.Bacc("TRN2", target_bir_lowering=False, num_devices=1)
    args = [nc.dram_tensor(n, v.shape, mb.dt.from_np(v.dtype), kind="ExternalInput").ap() for n, v in arrays.items()]
    args.append(nc.dram_tensor("out_h", (PAIRS, P, DIM), mb.dt.float32, kind="ExternalOutput").ap())
    build_program(nc, *args)
    r = run_bass_kernel_spmd(nc, [arrays], core_ids=[0])
    return r.results[0]["out_h"].reshape(IMAGES, TOKENS, DIM)
```
